# Optimizing a Trainium2 kernel written in Bass

```python
import numpy as np
import jax
import jax.numpy as jnp

def _softmax(x, axis=-1):
    return jax.nn.softmax(x, axis=axis)

def _gelu(x):
    return jax.nn.gelu(x, approximate=True)

def _silu(x):
    return jax.nn.silu(x)

def _sigmoid(x):
    return jax.nn.sigmoid(x)

def _layernorm(x, axis=-1, eps=1e-05):
    m = jnp.mean(x, axis=axis, keepdims=True)
    v = jnp.var(x, axis=axis, keepdims=True)
    return (x - m) / jnp.sqrt(v + eps)

def _scatter_add(tgt, idx, src, axis=0):
    return tgt.at[idx].add(src)

def _segment_sum(src, seg, n):
    return jax.ops.segment_sum(src, seg, n)
kernel_name = 'mk_seq_preln_d1_jaxref_r2_c3366b'

def setup_inputs(seed: int=0):
    np.random.seed(seed)
    _w = jnp.asarray

    def _L0_attn_setup():
        import jax, jax.numpy as jnp
        import numpy as np
        RSQRT2 = 2 ** (-0.5)
        B, S, D_IN = (2, 2048, 512)
        H, D_HEAD = (8, 64)
        QK_DIM = H * D_HEAD
        V_DIM = H * D_HEAD
        OUT_DIM = D_IN
        LN_EPS = 1e-05

        def _layernorm(y, gamma, beta):
            mu = jnp.mean(y, axis=-1, keepdims=True)
            var = jnp.mean(jnp.square(y - mu), axis=-1, keepdims=True)
            return (y - mu) * jax.lax.rsqrt(var + LN_EPS) * gamma + beta
        key = jax.random.key(seed)
        ks = jax.random.split(key, 8)

        def lecun(k, fan_in, shape):
            return jax.random.normal(k, shape, dtype=jnp.float32) * (1.0 / np.sqrt(fan_in))
        return {'x': jax.random.normal(ks[0], (B, S, D_IN), dtype=jnp.float32), 'W_qk': lecun(ks[1], D_IN, (D_IN, 2 * QK_DIM)), 'b_qk': jnp.zeros((2 * QK_DIM,), jnp.float32), 'W_v': lecun(ks[2], D_IN, (D_IN, V_DIM)), 'b_v': jnp.zeros((V_DIM,), jnp.float32), 'W_out': lecun(ks[3], V_DIM, (V_DIM, OUT_DIM)), 'b_out': jnp.zeros((OUT_DIM,), jnp.float32), 'ln_gamma': jnp.ones((OUT_DIM,), jnp.float32), 'ln_beta': jnp.zeros((OUT_DIM,), jnp.float32)}
    _L0_attn_in = _L0_attn_setup()

    def _L0_ffn_setup():
        import jax, jax.numpy as jnp
        import numpy as np
        DIM = 512

        def _reference_tuple_inner(x, W_r, W_k, W_v, mu_r, mu_k):
            B, T, C = x.shape
            x_prev = jnp.concatenate([jnp.zeros((B, 1, C), x.dtype), x[:, :-1, :]], axis=1)
            xr = mu_r * x + (1.0 - mu_r) * x_prev
            xk = mu_k * x + (1.0 - mu_k) * x_prev
            r = jax.nn.sigmoid(jnp.einsum('btc,dc->btd', xr, W_r))
            k = jnp.einsum('btc,dc->btd', xk, W_k)
            k_act = jnp.square(jax.nn.relu(k))
            out = r * jnp.einsum('btc,dc->btd', k_act, W_v)
            new_state = x[:, -1, :]
            return (out, new_state)
        key = jax.random.key(seed)
        ks = jax.random.split(key, 6)
        B, T, C = (8, 1024, DIM)
        x = jax.random.normal(ks[0], (B, T, C), dtype=jnp.float32)
        s = 1.0 / np.sqrt(C)
        W_r = jax.random.uniform(ks[1], (C, C), jnp.float32, -s, s)
        W_k = jax.random.uniform(ks[2], (C, C), jnp.float32, -s, s)
        W_v = jax.random.uniform(ks[3], (C, C), jnp.float32, -s, s)
        mu_r = jax.random.uniform(ks[4], (C,), jnp.float32)
        mu_k = jax.random.uniform(ks[5], (C,), jnp.float32)
        return {'x': x, 'W_r': W_r, 'W_k': W_k, 'W_v': W_v, 'mu_r': mu_r, 'mu_k': mu_k}
    _L0_ffn_in = _L0_ffn_setup()
    _d = {'L0_attn_x': _L0_attn_in['x'], 'L0_attn_W_qk': _L0_attn_in['W_qk'], 'L0_attn_b_qk': _L0_attn_in['b_qk'], 'L0_attn_W_v': _L0_attn_in['W_v'], 'L0_attn_b_v': _L0_attn_in['b_v'], 'L0_attn_W_out': _L0_attn_in['W_out'], 'L0_attn_b_out': _L0_attn_in['b_out'], 'L0_attn_ln_gamma': _L0_attn_in['ln_gamma'], 'L0_attn_ln_beta': _L0_attn_in['ln_beta'], 'L0_ffn_W_r': _L0_ffn_in['W_r'], 'L0_ffn_W_k': _L0_ffn_in['W_k'], 'L0_ffn_W_v': _L0_ffn_in['W_v'], 'L0_ffn_mu_r': _L0_ffn_in['mu_r'], 'L0_ffn_mu_k': _L0_ffn_in['mu_k']}
    _x0 = _d['L0_attn_x']
    _d['L0_attn_x'] = jax.random.normal(jax.random.fold_in(jax.random.key(seed), 1), (8, 1024, 512), dtype=_x0.dtype)
    del _x0
    return _d

def reference(L0_attn_x, L0_attn_W_qk, L0_attn_b_qk, L0_attn_W_v, L0_attn_b_v, L0_attn_W_out, L0_attn_b_out, L0_attn_ln_gamma, L0_attn_ln_beta, L0_ffn_W_r, L0_ffn_W_k, L0_ffn_W_v, L0_ffn_mu_r, L0_ffn_mu_k):

    def _L0_attn_ref(x, W_qk, b_qk, W_v, b_v, W_out, b_out, ln_gamma, ln_beta):
        import jax, jax.numpy as jnp
        import numpy as np
        RSQRT2 = 2 ** (-0.5)
        B, S, D_IN = (2, 2048, 512)
        H, D_HEAD = (8, 64)
        QK_DIM = H * D_HEAD
        V_DIM = H * D_HEAD
        OUT_DIM = D_IN
        LN_EPS = 1e-05

        def _layernorm(y, gamma, beta):
            mu = jnp.mean(y, axis=-1, keepdims=True)
            var = jnp.mean(jnp.square(y - mu), axis=-1, keepdims=True)
            return (y - mu) * jax.lax.rsqrt(var + LN_EPS) * gamma + beta
        b, s, _ = x.shape
        scale = D_HEAD ** (-0.5)
        qk = x @ W_qk + b_qk
        qk = qk.reshape(b, s, H, D_HEAD, 2)
        q, k = (qk[..., 0], qk[..., 1])
        v = (x @ W_v + b_v).reshape(b, s, H, D_HEAD)
        sim = jnp.einsum('bihd,bjhd->bhij', q, k) * scale
        attn = jax.nn.softmax(sim, axis=-1)
        o = jnp.einsum('bhij,bjhd->bihd', attn, v)
        o = o.reshape(b, s, V_DIM)
        y = _layernorm(o @ W_out + b_out, ln_gamma, ln_beta)
        return (y + x) * RSQRT2

    def _L0_ffn_ref(x, W_r, W_k, W_v, mu_r, mu_k):
        import jax, jax.numpy as jnp
        import numpy as np
        DIM = 512

        def _reference_tuple_inner(x, W_r, W_k, W_v, mu_r, mu_k):
            B, T, C = x.shape
            x_prev = jnp.concatenate([jnp.zeros((B, 1, C), x.dtype), x[:, :-1, :]], axis=1)
            xr = mu_r * x + (1.0 - mu_r) * x_prev
            xk = mu_k * x + (1.0 - mu_k) * x_prev
            r = jax.nn.sigmoid(jnp.einsum('btc,dc->btd', xr, W_r))
            k = jnp.einsum('btc,dc->btd', xk, W_k)
            k_act = jnp.square(jax.nn.relu(k))
            out = r * jnp.einsum('btc,dc->btd', k_act, W_v)
            new_state = x[:, -1, :]
            return (out, new_state)
        return _reference_tuple_inner(x, W_r, W_k, W_v, mu_r, mu_k)[0]
    x = L0_attn_x
    x = x + _L0_attn_ref(_layernorm(x, axis=-1), L0_attn_W_qk, L0_attn_b_qk, L0_attn_W_v, L0_attn_b_v, L0_attn_W_out, L0_attn_b_out, L0_attn_ln_gamma, L0_attn_ln_beta)
    x = x + _L0_ffn_ref(_layernorm(x, axis=-1), L0_ffn_W_r, L0_ffn_W_k, L0_ffn_W_v, L0_ffn_mu_r, L0_ffn_mu_k)
    return x

_drawn_inputs = setup_inputs


def setup_inputs(seed=0):
    import zlib

    import numpy as np

    out = dict(_drawn_inputs(seed))
    spreads = {'L0_attn_b_qk': (0.0, 0.493),
     'L0_attn_b_v': (0.0, 0.1),
     'L0_attn_b_out': (0.0, 0.1),
     'L0_attn_ln_gamma': (1.0, 0.2),
     'L0_attn_ln_beta': (0.0, 0.1)}
    factors = {'L0_ffn_W_r': 5.355, 'L0_ffn_mu_r': 8.0}
    for name, (base, spread) in spreads.items():
        noise = np.random.default_rng([zlib.crc32(name.encode()), seed]).standard_normal(out[name].shape)
        drawn = base * np.exp(spread * noise) if base else spread * noise
        out[name] = jnp.asarray(drawn.astype(out[name].dtype))
    for name, factor in factors.items():
        out[name] = (out[name] * factor).astype(out[name].dtype)
    return out
```

```python
from contextlib import ExitStack

import concourse.bass as bass
from concourse import mybir

F32 = mybir.dt.float32
F32R = mybir.dt.float32r
ALU = mybir.AluOpType
ACT = mybir.ActivationFunctionType
AX_X = mybir.AxisListType.X

P = 128
B, T, C = 8, 1024, 512
HEADS, DH = 8, 64
KC = C // P
TT = T // P
HALF = T // 2
SLOTS = HEADS * TT
LAST_SLOT = SLOTS + 6
XHAT_TURNS = [56, 57, 58, 59, 61, 62, 63, 64]
V_SLOTS = [0, 0, 1, 1, 2, 3, 4, 5]
QK_STORES = [3, 6]
NEXT_QK_STORES = [66, 70]
QUAD = 4
EPS = 1e-5
RSQRT2 = 2.0 ** -0.5
SCALE = DH ** -0.5


def f32(ap):
    return ap.bitcast(F32)


def query_tile(r):
    return r // 2 + (TT // 2) * (r % 2)


def attention_pass(nc, x, w_qk, b_qk, w_v, b_v, o_scratch, ln1_stats, ident):
    with ExitStack() as ctx:
        def sb(name, shape, dt=F32):
            return ctx.enter_context(nc.sbuf_tensor(name, shape, dt))

        def sem(name):
            return ctx.enter_context(nc.semaphore(name))

        wqk_hi = sb("wqk_hi", [P, KC, HEADS, 2, DH], F32R)
        wqk_lo = sb("wqk_lo", [P, KC, HEADS, 2, DH], F32R)
        wv_hi = sb("wv_hi", [P, KC, C], F32R)
        wv_lo = sb("wv_lo", [P, KC, C], F32R)
        bqk = sb("bqk", [P, HEADS])
        bv = sb("bv", [P, C])
        xT_hi = sb("xT_hi", [P, KC, T], F32R)
        xT_lo = sb("xT_lo", [P, KC, T], F32R)
        q_hilo = [sb(f"q_hilo{i}", [P, T], F32R) for i in range(2)]
        k_hihi = [sb(f"k_hihi{i}", [P, T], F32R) for i in range(2)]
        k_lolo = [sb(f"k_lolo{i}", [P, T], F32R) for i in range(2)]
        v = sb("v", [P, TT, C])
        probs = [sb(f"probs{i}", [P, T]) for i in range(3)]
        probsT = sb("probsT", [P, 2, TT, 2, 2 * P])
        neg_max = sb("neg_max", [P, 2, TT])
        row_sum = sb("row_sum", [P, 2, TT])
        row_inv = sb("row_inv", [P, 2, TT])
        inv_wide = sb("inv_wide", [P, 2, TT, DH])
        inv_cols = sb("inv_cols", [P, HALF])
        oT = [sb(f"oT{i}", [P, HALF]) for i in range(2)]
        xb = sb("xb", [P, TT, C])
        xhat = [sb(f"xhat{i}", [P, C]) for i in range(2)]
        bn6 = sb("bn6", [P, TT, 6])
        mean_var = sb("mean_var", [P, TT, 2])
        rstd = sb("rstd", [P, TT])
        neg_half = sb("neg_half", [P, TT])
        eps = sb("eps", [P, TT])
        wqk_raw = probsT[:, 0].rearrange("p a b c -> p (a b c)").rearrange("p (k h d s) -> p k h d s", k=KC, h=HEADS, s=2)
        wv_raw = probsT[:, 1].rearrange("p a b c -> p (a b c)")[:, 0:KC * C].rearrange("p (k n) -> p k n", k=KC)

        ps_scores = [ctx.enter_context(nc.psum_tensor(f"ps_scores{i}", [P, T], F32)) for i in range(2)]
        ps_turnA = ctx.enter_context(nc.psum_tensor("ps_turnA", [P, 4, P], F32))
        ps_turnB = ctx.enter_context(nc.psum_tensor("ps_turnB", [P, 4, P], F32))
        ps_o = ctx.enter_context(nc.psum_tensor("ps_o", [P, HALF], F32))
        ps_misc = ctx.enter_context(nc.psum_tensor("ps_misc", [P, HALF], F32))
        v_banks = [ps_turnA[:, :, :].rearrange("p a b -> p (a b)"), ps_turnB[:, :, :].rearrange("p a b -> p (a b)")] * 2
        v_banks = v_banks[0:3] + [ps_o[:, :]] * 5
        misc4 = ps_misc[:, :].rearrange("p (k n) -> p k n", k=KC)

        w_in = sem("w_in")
        w_split = sem("w_split")
        x_in = [sem(f"x_in{i}") for i in range(4)]
        bn_done = sem("bn_done")
        bn_step = sem("bn_step")
        eps_done = sem("eps_done")
        rstd_done = sem("rstd_done")
        half_set = sem("half_set")
        xhat_done = sem("xhat_done")
        xhatT_done = sem("xhatT_done")
        xT_hi_done = sem("xT_hi_done")
        xT_lo_done = sem("xT_lo_done")
        qk_done = sem("qk_done")
        qk_hi_done = sem("qk_hi_done")
        qk_lo_done = sem("qk_lo_done")
        k_copied = [sem(f"k_copied{i}") for i in range(2)]
        v_done = sem("v_done")
        v_stored = sem("v_stored")
        scores_done = sem("scores_done")
        max_done = sem("max_done")
        exp_done = sem("exp_done")
        turnA_done = sem("turnA_done")
        turnB_done = sem("turnB_done")
        turnA_stored = sem("turnA_stored")
        turnB_stored = sem("turnB_stored")
        pv_done = sem("pv_done")
        recip_done = sem("recip_done")
        inv_done = sem("inv_done")
        inv_turned = sem("inv_turned")
        inv_stored = sem("inv_stored")
        o_done = sem("o_done")
        oT_free = [sem(f"oT_free{i}") for i in range(2)]
        ident_set = sem("ident_set")
        stats_kept = sem("stats_kept")

        x_tiles = x.rearrange("b (t p) c -> b p t c", p=P)

        with nc.Block() as block:

            @block.sync
            def _(sp):
                sp.dma_start(wqk_raw, w_qk.rearrange("(k p) (h d s) -> p k h d s", p=P, h=HEADS, s=2)).then_inc(w_in, 16)
                sp.dma_start(wv_raw, w_v.rearrange("(k p) n -> p k n", p=P)).then_inc(w_in, 16)
                bqk_view = b_qk.rearrange("(h d s) -> s d h", h=HEADS, s=2)
                for s in range(2):
                    sp.dma_start(bqk[s * DH:(s + 1) * DH, :], bqk_view[s], allow_slow_non_contiguous=True).then_inc(w_in, 16)
                sp.dma_start(bv[:, :], b_v.rearrange("(o n) -> o n", o=1).broadcast_to([P, C])).then_inc(w_in, 16)

                def load_x(b, i):
                    sp.dma_start(xb[:, 2 * i:2 * i + 2, :], x_tiles[b][:, 2 * i:2 * i + 2, :]).then_inc(x_in[i], 16)

                def copy_k(b, h):
                    sp.wait_ge(qk_lo_done, 16 * b + 2 * h + 2)
                    sp.dma_start(f32(k_hihi[h % 2][0:DH, :]), f32(k_hihi[h % 2][DH:P, :])).then_inc(k_copied[h % 2], 16)
                    sp.dma_start(f32(k_lolo[h % 2][0:DH, :]), f32(k_lolo[h % 2][DH:P, :])).then_inc(k_copied[h % 2], 16)

                def store_o(b, h):
                    sp.wait_ge(o_done, 8 * b + h + 1)
                    for half in range(2):
                        sp.dma_start(o_scratch[b][half, h, :, :],
                                     oT[h % 2][half * DH:(half + 1) * DH, :]).then_inc(oT_free[h % 2], 16)

                for i in range(4):
                    load_x(0, i)
                copy_k(0, 0)

                def entry(b, last):
                    for h in range(HEADS + 1):
                        if h == 0 and not last:
                            sp.wait_ge(xhat_done, 8 * b + 8)
                        if h < 4 and not last:
                            load_x(b + 1, h)
                        if h < HEADS - 1:
                            copy_k(b, h + 1)
                        if h == HEADS and not last:
                            copy_k(b + 1, 0)
                        if h >= 1:
                            store_o(b, h - 1)

                with sp.Fori(0, B - 1) as b:
                    entry(b, False)
                entry(B - 1, True)
                for i in range(2):
                    sp.wait_ge(oT_free[i], 16 + 128 * B)

            @block.gpsimd
            def _(pool):
                pool.memset(ident[:, :], 0.0).then_inc(ident_set, 1)
                pool.wait_ge(ident_set, 1)
                pool.affine_select(out=ident[:, :], in_=ident[:, :], compare_op=ALU.not_equal, fill=1.0, base=0,
                                   pattern=[[-1, P]], channel_multiplier=1).then_inc(ident_set, 1)
                pool.memset(neg_half[:, :], -0.5).then_inc(half_set, 1)
                pool.memset(eps[:, :], EPS).then_inc(half_set, 1)
                pool.wait_ge(half_set, 2)

                def rstd_of(b):
                    pool.wait_ge(bn_done, b + 1)
                    pool.tensor_tensor(rstd[:, :], mean_var[:, :, 1], eps[:, :], ALU.add).then_inc(eps_done, 1)
                    pool.wait_ge(eps_done, b + 1)
                    pool.tensor_tensor(rstd[:, :], rstd[:, :], neg_half[:, :], ALU.pow).then_inc(rstd_done, 1)

                rstd_of(0)
                with pool.Fori(0, B - 1) as b:
                    rstd_of(b + 1)

            @block.vector
            def _(dve):
                for i in range(2):
                    dve.memset(oT[i][:, :], 0.0).then_inc(oT_free[i], 16)
                dve.wait_ge(w_in, 80)
                steps = 0
                for kc in range(KC):
                    for s, scale in enumerate((SCALE, 1.0)):
                        raw = wqk_raw[:, kc, :, :, s]
                        dve.tensor_scalar(wqk_hi[:, kc, :, s, :], raw, scale, None, ALU.mult).then_inc(w_split, 1)
                        steps += 1
                        dve.wait_ge(w_split, steps)
                        dve.scalar_tensor_tensor(wqk_lo[:, kc, :, s, :], raw, scale, f32(wqk_hi[:, kc, :, s, :]),
                                                 ALU.mult, ALU.subtract).then_inc(w_split, 1)
                        steps += 1
                dve.tensor_copy(wv_hi[:, :, :], wv_raw).then_inc(w_split, 1)
                dve.tensor_scalar(bqk[0:DH, :], bqk[0:DH, :], SCALE, None, ALU.mult).then_inc(w_split, 1)
                dve.wait_ge(w_split, steps + 2)
                dve.tensor_tensor(wv_lo[:, :, :], wv_raw, f32(wv_hi[:, :, :]), ALU.subtract).then_inc(w_split, 1)

                def stats(b, t):
                    dve.wait_ge(x_in[t // 2], 16 * b + 16)
                    dve.bn_stats(bn6[:, t, :], xb[:, t, :]).then_inc(bn_step, 1)

                def aggregate():
                    for t in range(TT):
                        ins = dve.bn_aggr(mean_var[:, t, :], bn6[:, t, :])
                    ins.then_inc(bn_done, 1)

                def keep_stats(b):
                    dve.wait_ge(rstd_done, b + 1)
                    dve.tensor_copy(ln1_stats[:, bass.ds(b * TT, TT), 0], mean_var[:, :, 0])
                    dve.tensor_copy(ln1_stats[:, bass.ds(b * TT, TT), 1], rstd[:, :]).then_inc(stats_kept, 1)

                def normalise(b, t):
                    if t >= 2:
                        dve.wait_ge(xhatT_done, 8 * b + t - 1)
                    dve.tensor_scalar(xhat[t % 2][:, :], xb[:, t, :], mean_var[:, t, 0:1], rstd[:, t:t + 1],
                                      ALU.subtract, ALU.mult).then_inc(xhat_done, 1)

                def store_xT_lo(b, t):
                    dve.wait_ge(xT_hi_done, 8 * b + t + 1)
                    cols = slice(t * P, (t + 1) * P)
                    dve.tensor_tensor(xT_lo[:, :, cols], misc4, f32(xT_hi[:, :, cols]),
                                      ALU.subtract).then_inc(xT_lo_done, 1)

                def store_qk_lo(b, h, half):
                    dve.wait_ge(qk_hi_done, 16 * b + 2 * h + half + 1)
                    cols = slice(half * HALF, (half + 1) * HALF)
                    i = h % 2
                    dve.scalar_tensor_tensor(q_hilo[i][DH:P, cols], ps_misc[0:DH, :], bqk[0:DH, h:h + 1],
                                             f32(q_hilo[i][0:DH, cols]), ALU.add, ALU.subtract)
                    dve.scalar_tensor_tensor(k_lolo[i][DH:P, cols], ps_misc[DH:P, :], bqk[DH:P, h:h + 1],
                                             f32(k_hihi[i][DH:P, cols]), ALU.add, ALU.subtract).then_inc(qk_lo_done, 1)

                for t in range(TT):
                    stats(0, t)
                dve.wait_ge(bn_step, TT)
                aggregate()
                keep_stats(0)
                for t in range(TT):
                    normalise(0, t)
                    if t >= 1:
                        store_xT_lo(0, t - 1)
                store_xT_lo(0, TT - 1)
                for half in range(2):
                    store_qk_lo(0, 0, half)

                def entry(b, last):
                    for n in range(LAST_SLOT + 1):
                        h, r = n // TT, n % TT
                        if n == 6 * TT and not last:
                            dve.wait_ge(bn_step, 8 * b + 16)
                        if n < SLOTS:
                            dve.wait_ge(scores_done, 64 * b + n + 1)
                            dve.tensor_reduce(neg_max[:, h % 2, r:r + 1], ps_scores[n % 2][:, :], AX_X, ALU.max,
                                              negate=True).then_inc(max_done, 1)
                        for t in range(TT):
                            if V_SLOTS[t] == n:
                                dve.wait_ge(v_done, 8 * b + t + 1)
                                dve.tensor_tensor(v[:, t, :], v_banks[t], bv[:, :], ALU.add).then_inc(v_stored, 1)
                        if r == 1 and h >= 1:
                            dve.wait_ge(exp_done, 64 * b + 8 * h)
                            dve.reciprocal(row_inv[:, (h - 1) % 2, :], row_sum[:, (h - 1) % 2, :]).then_inc(recip_done, 1)
                            dve.wait_ge(recip_done, 8 * b + h)
                            dve.tensor_copy(inv_wide[:, (h - 1) % 2, :, :],
                                            row_inv[:, (h - 1) % 2, :].unsqueeze(2).broadcast_to([P, TT, DH])).then_inc(inv_done, 1)
                        if r in QK_STORES and h < HEADS - 1:
                            store_qk_lo(b, h + 1, QK_STORES.index(r))
                        if n in NEXT_QK_STORES and not last:
                            store_qk_lo(b + 1, 0, NEXT_QK_STORES.index(n))
                        if not last:
                            if h == 5:
                                stats(b + 1, r)
                            if h == 6 and r == 0:
                                aggregate()
                            if h == 6 and r == 5:
                                keep_stats(b + 1)
                            if h == 6 and r >= 6:
                                normalise(b + 1, r - 6)
                            if n - 1 in XHAT_TURNS:
                                t = XHAT_TURNS.index(n - 1)
                                store_xT_lo(b + 1, t)
                                if t + 2 < TT:
                                    normalise(b + 1, t + 2)
                        if 2 <= n < SLOTS + 2:
                            m = n - 2
                            dve.wait_ge(turnB_done, 64 * b + m + 1)
                            dve.tensor_copy(probsT[:, m // QUAD % 2, 4:8, m % 2, m % QUAD // 2 * P:(m % QUAD // 2 + 1) * P],
                                            ps_turnB[:, :, :]).then_inc(turnB_stored, 1)
                        if r == 5 and h >= 1:
                            dve.wait_ge(pv_done, 8 * b + h)
                            dve.wait_ge(inv_stored, 8 * b + h)
                            dve.wait_ge(oT_free[(h - 1) % 2], 128 * b + 16 + 32 * ((h - 1) // 2))
                            dve.tensor_tensor(oT[(h - 1) % 2][:, :], ps_o[:, :], inv_cols[:, :],
                                              ALU.mult).then_inc(o_done, 1)

                with dve.Fori(0, B - 1) as b:
                    entry(b, False)
                entry(B - 1, True)

            @block.scalar
            def _(act):
                def store_xT_hi(b, t):
                    act.wait_ge(xhatT_done, 8 * b + t + 1)
                    act.activation(xT_hi[:, :, t * P:(t + 1) * P], misc4, ACT.Copy).then_inc(xT_hi_done, 1)

                def store_qk_hi(b, h, half):
                    act.wait_ge(qk_done, 16 * b + 2 * h + half + 1)
                    cols = slice(half * HALF, (half + 1) * HALF)
                    i = h % 2
                    act.activation(q_hilo[i][0:DH, cols], ps_misc[0:DH, :], ACT.Identity, bias=bqk[0:DH, h:h + 1])
                    act.activation(k_hihi[i][DH:P, cols], ps_misc[DH:P, :], ACT.Identity,
                                   bias=bqk[DH:P, h:h + 1]).then_inc(qk_hi_done, 1)

                def store_inv(b, h):
                    act.wait_ge(inv_turned, 8 * b + h)
                    if h >= 2:
                        act.wait_ge(o_done, 8 * b + h - 1)
                    act.activation(inv_cols[:, :], ps_misc[:, :], ACT.Copy).then_inc(inv_stored, 1)

                for t in range(TT):
                    store_xT_hi(0, t)
                for half in range(2):
                    store_qk_hi(0, 0, half)

                def entry(b, last):
                    for n in range(LAST_SLOT + 1):
                        h, r = n // TT, n % TT
                        if 1 <= n <= SLOTS:
                            m = n - 1
                            act.wait_ge(max_done, 64 * b + m + 1)
                            if m >= 3:
                                act.wait_ge(turnB_done, 64 * b + m - 2)
                            act.activation(probs[m % 3][:, :], ps_scores[m % 2][:, :], ACT.Exp,
                                           bias=neg_max[:, m // TT % 2, m % TT:m % TT + 1],
                                           accum_out=row_sum[:, m // TT % 2, m % TT:m % TT + 1]).then_inc(exp_done, 1)
                        if n == 61:
                            store_inv(b, 7)
                        if r in QK_STORES and h < HEADS - 1:
                            store_qk_hi(b, h + 1, QK_STORES.index(r))
                        if n in NEXT_QK_STORES and not last:
                            store_qk_hi(b + 1, 0, NEXT_QK_STORES.index(n))
                        if not last and n - 1 in XHAT_TURNS:
                            store_xT_hi(b + 1, XHAT_TURNS.index(n - 1))
                        if 2 <= n < SLOTS + 2:
                            m = n - 2
                            act.wait_ge(turnA_done, 64 * b + m + 1)
                            act.activation(probsT[:, m // QUAD % 2, 0:4, m % 2, m % QUAD // 2 * P:(m % QUAD // 2 + 1) * P],
                                           ps_turnA[:, :, :], ACT.Copy).then_inc(turnA_stored, 1)
                        if r == 4 and h >= 1 and n != 60:
                            store_inv(b, h)

                with act.Fori(0, B - 1) as b:
                    entry(b, False)
                entry(B - 1, True)

            @block.tensor
            def _(pe):
                def turn_xhat(b, t):
                    pe.wait_ge(xhat_done, 8 * b + t + 1)
                    for k in range(KC):
                        ins = pe.transpose(misc4[:, k, :], xhat[t % 2][:, k * P:(k + 1) * P], ident[:, :])
                    ins.then_inc(xhatT_done, 1)

                def project_qk(b, h, half, first, end):
                    cols = slice(half * HALF, (half + 1) * HALF)
                    prods = [(w, xt, kc) for kc in range(KC) for w, xt in ((wqk_lo, xT_hi), (wqk_hi, xT_lo), (wqk_hi, xT_hi))]
                    for n in range(first, end):
                        w, xt, kc = prods[n]
                        ins = pe.matmul(ps_misc[:, :], w[:, kc, h, :, :].rearrange("p s d -> p (s d)"), xt[:, kc, cols],
                                        start=(n == 0), stop=(n == 11))
                    if end == 12:
                        ins.then_inc(qk_done, 1)

                def misc_free_of_qk(b, h, half):
                    pe.wait_ge(qk_hi_done, 16 * b + 2 * h + half + 1)
                    pe.wait_ge(qk_lo_done, 16 * b + 2 * h + half + 1)

                def misc_free_of_xhat(b, t):
                    pe.wait_ge(xT_hi_done, 8 * b + t + 1)
                    pe.wait_ge(xT_lo_done, 8 * b + t + 1)

                pe.wait_ge(ident_set, 2)
                for t in range(TT):
                    if t >= 1:
                        misc_free_of_xhat(0, t - 1)
                    turn_xhat(0, t)
                misc_free_of_xhat(0, TT - 1)
                pe.wait_ge(w_split, 4 * KC + 3)
                project_qk(0, 0, 0, 0, 12)
                misc_free_of_qk(0, 0, 0)
                project_qk(0, 0, 1, 0, 12)

                def project_v(b, t):
                    prods = [(xt, w, kc) for kc in range(KC) for xt, w in ((xT_lo, wv_hi), (xT_hi, wv_lo), (xT_hi, wv_hi))]
                    for i, (xt, w, kc) in enumerate(prods):
                        ins = pe.matmul(v_banks[t], xt[:, kc, t * P:(t + 1) * P], w[:, kc, :], start=(i == 0), stop=(i == 11))
                    ins.then_inc(v_done, 1)

                def scores(b, n):
                    h, r = n // TT, n % TT
                    if r == 0:
                        pe.wait_ge(qk_lo_done, 16 * b + 2 * h + 2)
                        pe.wait_ge(k_copied[h % 2], 128 * b + 32 * (h // 2) + 32)
                    if n >= 2:
                        pe.wait_ge(exp_done, 64 * b + n - 1)
                    tile = slice(query_tile(r) * P, (query_tile(r) + 1) * P)
                    for half in range(2):
                        cols = slice(half * HALF, (half + 1) * HALF)
                        for i, k in enumerate((k_lolo, k_hihi)):
                            ins = pe.matmul(ps_scores[n % 2][:, cols], q_hilo[h % 2][:, tile], k[h % 2][:, cols],
                                            start=(i == 0), stop=(i == 1))
                    ins.then_inc(scores_done, 1)

                def turn_probs(b, m):
                    pe.wait_ge(exp_done, 64 * b + m + 1)
                    for ps, first, stored, done in ((ps_turnA, 0, turnA_stored, turnA_done),
                                                    (ps_turnB, 4, turnB_stored, turnB_done)):
                        if m >= 1:
                            pe.wait_ge(stored, 64 * b + m)
                        for j in range(4):
                            ins = pe.transpose(ps[:, j, :], probs[m % 3][:, (first + j) * P:(first + j + 1) * P], ident[:, :])
                        ins.then_inc(done, 1)

                def p_at_v(b, quad, part):
                    h, q2 = quad // 2, quad % 2
                    if part == 0:
                        pe.wait_ge(turnA_stored, 64 * b + QUAD * quad + QUAD)
                        pe.wait_ge(turnB_stored, 64 * b + QUAD * quad + QUAD)
                        if q2 == 0 and h >= 1:
                            pe.wait_ge(o_done, 8 * b + h)
                    for jt in (2 * part, 2 * part + 1):
                        for half in range(2):
                            ins = pe.matmul(ps_o[half * DH:(half + 1) * DH, q2 * 2 * P:(q2 + 1) * 2 * P],
                                            v[:, jt, h * DH:(h + 1) * DH], probsT[:, quad % 2, jt, half, :],
                                            start=(jt == 0), stop=(jt == TT - 1))
                    if part == 3 and q2 == 1:
                        ins.then_inc(pv_done, 1)

                def spread_inv(b, h):
                    pe.wait_ge(inv_done, 8 * b + h + 1)
                    for m in range(4):
                        cols = inv_wide[:, h % 2, 2 * m:2 * m + 2, :].rearrange("p r d -> p (r d)")
                        ins = pe.transpose(ps_misc[:, m * P:(m + 1) * P], cols, ident[:, :])
                    ins.then_inc(inv_turned, 1)

                def entry(b, last):
                    for n in range(LAST_SLOT):
                        h, r = n // TT, n % TT
                        if n < SLOTS:
                            scores(b, n)
                        for t in range(TT):
                            if V_SLOTS[t] == n:
                                if t in (2, 4, 5, 6, 7):
                                    pe.wait_ge(v_stored, 8 * b + (1 if t == 2 else t))
                                project_v(b, t)
                        if r == 4 and 1 <= h < HEADS - 1:
                            misc_free_of_qk(b, h + 1, 0)
                            spread_inv(b, h - 1)
                        if n == SLOTS + 4:
                            if not last:
                                misc_free_of_qk(b + 1, 0, 0)
                            spread_inv(b, HEADS - 1)
                        if n == 2:
                            pe.wait_ge(v_stored, 8 * b + 3)
                        if 2 <= n < SLOTS + 2:
                            turn_probs(b, n - 2)
                        if n == 6:
                            pe.wait_ge(v_stored, 8 * b + TT)
                        if n >= 6:
                            p_at_v(b, (n - 6) // QUAD, (n - 6) % QUAD)
                        if h < HEADS - 1:
                            if r == 0:
                                misc_free_of_qk(b, h, 1)
                                project_qk(b, h + 1, 0, 0, 4)
                            if r == 1:
                                project_qk(b, h + 1, 0, 4, 8)
                            if r == 2:
                                project_qk(b, h + 1, 0, 8, 12)
                            if r == 4:
                                misc_free_of_qk(b, h + 1, 0)
                                if h >= 1:
                                    pe.wait_ge(inv_stored, 8 * b + h)
                                project_qk(b, h + 1, 1, 0, 6)
                            if r == 5:
                                project_qk(b, h + 1, 1, 6, 12)
                        if n == 60:
                            if last:
                                misc_free_of_qk(b, h, 1)
                            else:
                                misc_free_of_xhat(b + 1, 3)
                            spread_inv(b, h - 1)
                        if not last and n in XHAT_TURNS:
                            t = XHAT_TURNS.index(n)
                            if t == 0:
                                misc_free_of_qk(b, h, 1)
                            else:
                                misc_free_of_xhat(b + 1, t - 1)
                            if t == 4:
                                pe.wait_ge(inv_stored, 8 * b + h)
                            turn_xhat(b + 1, t)
                        if not last:
                            if n == 65:
                                misc_free_of_xhat(b + 1, TT - 1)
                                project_qk(b + 1, 0, 0, 0, 12)
                            if n == 68:
                                pe.wait_ge(inv_stored, 8 * b + h)
                                project_qk(b + 1, 0, 1, 0, 6)
                            if n == 69:
                                project_qk(b + 1, 0, 1, 6, 12)

                with pe.Fori(0, B - 1) as b:
                    entry(b, False)
                entry(B - 1, True)


def mix_pass(nc, x, o_scratch, w_out, b_out, gamma, beta, w_r, w_k, w_v, mu_r, mu_k, out, ln1_stats, ident):
    with ExitStack() as ctx:
        def sb(name, shape, dt=F32):
            return ctx.enter_context(nc.sbuf_tensor(name, shape, dt))

        def sem(name):
            return ctx.enter_context(nc.semaphore(name))

        CHUNK = T // 2
        NT = CHUNK // P
        CHUNKS = B * 2
        NAMES = ("out", "r", "k", "v")

        hi = {n: sb(f"mix_w{n}_hi", [P, KC, C], F32R) for n in NAMES}
        lo = {n: sb(f"mix_w{n}_lo", [P, KC, C], F32R) for n in NAMES}
        gam = sb("gam", [P, C])
        bet = sb("bet", [P, C])
        bo = sb("bo", [P, C])
        mu = {"k": sb("mu_k", [P, KC]), "r": sb("mu_r", [P, KC])}
        mu1 = {"k": sb("mu1_k", [P, KC]), "r": sb("mu1_r", [P, KC])}
        neg_half = sb("neg_half2", [P, NT])
        eps = sb("eps2", [P, NT])
        st1 = sb("st1", [P, NT, 2])
        xs = sb("xs", [P, NT, 2])
        o_raw = sb("o_raw", [P, KC, CHUNK])
        o_hi = sb("o_hi", [P, KC, CHUNK], F32R)
        o_lo = sb("o_lo", [P, KC, CHUNK], F32R)
        xc = sb("xc", [P, NT, C])
        y = sb("y", [P, NT, C])
        x2 = [sb(f"x2_{i}", [P, NT, C]) for i in range(2)]
        bn6 = sb("bn6b", [P, NT, 6])
        mv_y = sb("mv_y", [P, NT, 2])
        mv_2 = sb("mv_2", [P, NT, 2])
        rstd_y = sb("rstd_y", [P, NT])
        rstd_2 = sb("rstd_2", [P, NT])
        lnT = sb("lnT", [P, KC, CHUNK + 1])
        mixed = sb("mixed", [P, KC, CHUNK])
        m_hi = {n: sb(f"m{n}_hi", [P, KC, CHUNK], F32R) for n in "kr"}
        m_lo = {n: sb(f"m{n}_lo", [P, KC, CHUNK], F32R) for n in "kr"}
        relu = sb("relu", [P, 2, CHUNK])
        act_hi = sb("act_hi", [P, KC, CHUNK], F32R)
        act_lo = sb("act_lo", [P, KC, CHUNK], F32R)
        gate = sb("gate", [P, NT, C])
        raw = {"out": o_raw, "r": mixed, "k": y, "v": gate}

        bank = [ctx.enter_context(nc.psum_tensor(f"bank{i}", [P, C], F32)) for i in range(8)]
        ps_y, ps_k, ps_r, ps_v = bank[0:2], bank[2:4], bank[4:6], bank[6:8]

        w_in = [sem(f"wc_in{i}") for i in range(5)]
        small_set = sem("small_set")
        w_turned = sem("w_turned")
        w_hi_done = sem("w_hi_done")
        w_lo_done = sem("w_lo_done")
        wo_split = sem("wo_split")
        o_in = sem("o_in")
        x_in = sem("xc_in")
        o_hi_done = sem("o_hi_done")
        o_lo_done = sem("o_lo_done")
        y_done = sem("y_done")
        y_stored = sem("y_stored")
        bn_step = sem("bn_step2")
        bn_y = sem("bn_y")
        eps_step = sem("eps_step")
        rstd_y_done = sem("rstd_y_done")
        xs_step = sem("xs_step")
        xs_done = sem("xs_done")
        res_act = sem("res_act")
        res_done = sem("res_done")
        t1_done = sem("t1_done")
        x2_done = sem("x2_done")
        bn2_step = sem("bn2_step")
        bn_2 = sem("bn_2")
        rstd_2_done = sem("rstd_2_done")
        ln2_done = sem("ln2_done")
        ln2_turned = sem("ln2_turned")
        prev_done = sem("prev_done")
        lnT_done = sem("lnT_done")
        before_done = {n: sem(f"before_{n}") for n in "kr"}
        mixed_done = {n: sem(f"mixed_{n}") for n in "kr"}
        m_hi_done = {n: sem(f"m_hi_{n}") for n in "kr"}
        m_lo_done = {n: sem(f"m_lo_{n}") for n in "kr"}
        k_done = sem("k_done")
        relu_done = sem("relu_done")
        act_hi_done = sem("act_hi_done")
        sq_done = sem("sq_done")
        act_lo_done = sem("act_lo_done")
        r_done = sem("r_done")
        gate_done = sem("gate_done")
        kv_done = sem("kv_done")
        rkv_done = sem("rkv_done")
        sum_done = sem("sum_done")
        out_done = sem("out_done")

        o_view = o_scratch.rearrange("b c h d t -> (b c) (h d) t").rearrange("g (k p) t -> g p k t", p=P)
        x_view = x.rearrange("b (c t p) n -> (b c) p t n", c=2, p=P)
        out_view = out.rearrange("b (c t p) n -> (b c) p t n", c=2, p=P)

        def spread(vec):
            return vec.rearrange("(o n) -> o n", o=1).broadcast_to([P, C])

        def over_steps(eng, step):
            step(0, 0, True, False)
            with eng.Fori(0, CHUNKS // 2 - 1) as i:
                step(2 * i + 1, 1, True, True)
                step(2 * i + 2, 0, True, True)
            step(CHUNKS - 1, 1, True, True)
            step(CHUNKS, 0, False, True)

        with nc.Block() as block:

            @block.sync
            def _(sp):
                for i, (n, w) in enumerate((("out", w_out), ("r", w_r), ("k", w_k), ("v", w_v))):
                    sp.dma_start(raw[n][:, :, :], w.rearrange("(k p) n -> p k n", p=P)).then_inc(w_in[i], 16)
                for dst, src in ((gam, gamma), (bet, beta), (bo, b_out)):
                    sp.dma_start(dst[:, :], spread(src)).then_inc(w_in[4], 16)
                for dst, src in ((mu["k"], mu_k), (mu["r"], mu_r)):
                    sp.dma_start(dst[:, :], src.rearrange("(k p) -> p k", p=P),
                                 allow_slow_non_contiguous=True).then_inc(w_in[4], 16)

                def load_o(g):
                    sp.dma_start(o_raw[:, :, :], o_view[g]).then_inc(o_in, 16)

                def load_x(g):
                    sp.dma_start(xc[:, :, :], x_view[g]).then_inc(x_in, 16)

                sp.wait_ge(wo_split, 2)
                load_o(0)
                load_x(0)

                def step(g, par, first, second):
                    if first and not (isinstance(g, int) and g == CHUNKS - 1):
                        sp.wait_ge(o_lo_done, g + 1)
                        load_o(g + 1)
                        sp.wait_ge(x2_done, 4 * g + 4)
                        load_x(g + 1)
                    if second:
                        for t in range(NT):
                            sp.wait_ge(sum_done, 4 * g - 3 + t)
                            sp.dma_start(out_view[g - 1][:, t, :], gate[:, t, :]).then_inc(out_done, 16)

                over_steps(sp, step)
                sp.wait_ge(out_done, 16 * NT * CHUNKS)

            @block.gpsimd
            def _(pool):
                pool.memset(eps[:, :], EPS).then_inc(eps_step, 1)
                pool.memset(neg_half[:, :], -0.5).then_inc(eps_step, 1)
                pool.wait_ge(eps_step, 2)
                pool.wait_ge(small_set, 2)

                def step(g, par, first, second):
                    if first:
                        pool.wait_ge(bn_y, g + 1)
                        pool.tensor_tensor(rstd_y[:, :], mv_y[:, :, 1], eps[:, :], ALU.add).then_inc(eps_step, 1)
                        pool.wait_ge(eps_step, 2 * g + 3)
                        pool.tensor_tensor(rstd_y[:, :], rstd_y[:, :], neg_half[:, :], ALU.pow).then_inc(rstd_y_done, 1)
                        for t in range(NT):
                            pool.wait_ge(res_act, 4 * g + t + 1)
                            pool.tensor_tensor(xc[:, t, :], xc[:, t, :], bet[:, :], ALU.add).then_inc(res_done, 1)
                        pool.wait_ge(bn_2, g + 1)
                        pool.tensor_tensor(rstd_2[:, :], mv_2[:, :, 1], eps[:, :], ALU.add).then_inc(eps_step, 1)
                        pool.wait_ge(eps_step, 2 * g + 4)
                        pool.tensor_tensor(rstd_2[:, :], rstd_2[:, :], neg_half[:, :], ALU.pow).then_inc(rstd_2_done, 1)
                    if second:
                        for t in range(NT):
                            pool.wait_ge(rkv_done, 4 * g - 3 + t)
                            pool.tensor_tensor(gate[:, t, :], gate[:, t, :], x2[1 - par][:, t, :],
                                               ALU.add).then_inc(sum_done, 1)

                over_steps(pool, step)

            @block.vector
            def _(dve):
                dve.wait_ge(w_in[4], 80)
                dve.tensor_scalar(gam[:, :], gam[:, :], RSQRT2, None, ALU.mult).then_inc(small_set, 1)
                dve.tensor_scalar(bet[:, :], bet[:, :], RSQRT2, None, ALU.mult).then_inc(small_set, 1)
                for n in "kr":
                    dve.tensor_scalar(mu1[n][:, :], mu[n][:, :], -1.0, 1.0, ALU.mult, ALU.add).then_inc(small_set, 1)
                dve.memset(lnT[:, :, 0:1], 0.0).then_inc(small_set, 1)
                dve.wait_ge(w_in[0], 16)
                dve.tensor_copy(hi["out"][:, :, :], raw["out"][:, :, :]).then_inc(wo_split, 1)
                dve.wait_ge(wo_split, 1)
                dve.tensor_tensor(lo["out"][:, :, :], raw["out"][:, :, :], f32(hi["out"][:, :, :]),
                                  ALU.subtract).then_inc(wo_split, 1)
                for i, n in enumerate(("r", "k", "v")):
                    for kc in range(KC):
                        u = KC * i + kc
                        dve.wait_ge(w_hi_done, u + 1)
                        dve.tensor_tensor(lo[n][:, kc, :], bank[u % 8][:, :], f32(hi[n][:, kc, :]),
                                          ALU.subtract).then_inc(w_lo_done, 1)

                def residual_scales(g):
                    dve.tensor_scalar(xs[:, :, 0], ln1_stats[:, bass.ds(g * NT, NT), 1], RSQRT2, None,
                                      ALU.mult).then_inc(xs_step, 1)
                    dve.tensor_copy(st1[:, :, 0], ln1_stats[:, bass.ds(g * NT, NT), 0]).then_inc(xs_step, 1)
                    dve.wait_ge(xs_step, 3 * g + 2)
                    dve.scalar_tensor_tensor(xs[:, :, 1], st1[:, :, 0], -1.0, xs[:, :, 0], ALU.mult,
                                             ALU.mult).then_inc(xs_step, 1)
                    dve.wait_ge(xs_step, 3 * g + 3)
                    dve.tensor_scalar(xs[:, :, 0], xs[:, :, 0], 1.0, None, ALU.add).then_inc(xs_done, 1)

                def split_o(g):
                    dve.wait_ge(o_hi_done, g + 1)
                    dve.tensor_tensor(o_lo[:, :, :], o_raw[:, :, :], f32(o_hi[:, :, :]), ALU.subtract).then_inc(o_lo_done, 1)

                def store_y(g, t):
                    dve.wait_ge(y_done, 4 * g + t + 1)
                    dve.tensor_tensor(y[:, t, :], ps_y[t % 2][:, :], bo[:, :], ALU.add).then_inc(y_stored, 1)
                    dve.wait_ge(y_stored, 4 * g + t + 1)
                    dve.bn_stats(bn6[:, t, :], y[:, t, :]).then_inc(bn_step, 1)

                def aggregate(mv, done):
                    for t in range(NT):
                        ins = dve.bn_aggr(mv[:, t, :], bn6[:, t, :])
                    ins.then_inc(done, 1)

                def residual(g, par, t):
                    dve.scalar_tensor_tensor(y[:, t, :], y[:, t, :], mv_y[:, t, 0:1], gam[:, :], ALU.subtract,
                                             ALU.mult).then_inc(t1_done, 1)
                    dve.wait_ge(res_done, 4 * g + t + 1)
                    dve.wait_ge(t1_done, 4 * g + t + 1)
                    dve.scalar_tensor_tensor(x2[par][:, t, :], y[:, t, :], rstd_y[:, t:t + 1], xc[:, t, :], ALU.mult,
                                             ALU.add).then_inc(x2_done, 1)
                    dve.wait_ge(x2_done, 4 * g + t + 1)
                    dve.bn_stats(bn6[:, t, :], x2[par][:, t, :]).then_inc(bn2_step, 1)

                def activation_lo(f, d):
                    dve.wait_ge(act_hi_done, 4 * f + d + 1)
                    dve.tensor_tensor(relu[:, d % 2, :], relu[:, d % 2, :], relu[:, d % 2, :], ALU.mult).then_inc(sq_done, 1)
                    dve.wait_ge(sq_done, 4 * f + d + 1)
                    dve.tensor_tensor(act_lo[:, d, :], relu[:, d % 2, :], f32(act_hi[:, d, :]),
                                      ALU.subtract).then_inc(act_lo_done, 1)

                def gated(f, t):
                    dve.wait_ge(kv_done, 4 * f + t + 1)
                    dve.wait_ge(gate_done, 4 * f + t + 1)
                    dve.tensor_tensor(gate[:, t, :], ps_v[t % 2][:, :], gate[:, t, :], ALU.mult).then_inc(rkv_done, 1)

                def mix(g, n):
                    for kc in range(KC):
                        dve.wait_ge(before_done[n], 4 * g + kc + 1)
                        dve.scalar_tensor_tensor(mixed[:, kc, :], lnT[:, kc, 1:CHUNK + 1], mu[n][:, kc:kc + 1],
                                                 mixed[:, kc, :], ALU.mult, ALU.add).then_inc(mixed_done[n], 1)

                def mix_lo(g, n):
                    for kc in range(KC):
                        dve.wait_ge(m_hi_done[n], 4 * g + kc + 1)
                        dve.tensor_tensor(m_lo[n][:, kc, :], mixed[:, kc, :], f32(m_hi[n][:, kc, :]),
                                          ALU.subtract).then_inc(m_lo_done[n], 1)

                residual_scales(0)
                split_o(0)

                def step(g, par, first, second):
                    f = g - 1
                    if first:
                        for t in range(NT):
                            store_y(g, t)
                        dve.wait_ge(bn_step, 4 * g + 4)
                    if second:
                        activation_lo(f, 0)
                    if first:
                        aggregate(mv_y, bn_y)
                    if second:
                        activation_lo(f, 1)
                    if first:
                        dve.wait_ge(rstd_y_done, g + 1)
                    for t in range(NT):
                        if first:
                            residual(g, par, t)
                        if first and t == 3:
                            dve.wait_ge(bn2_step, 4 * g + 4)
                        if second and t >= 2:
                            activation_lo(f, t)
                        if first and t == 3:
                            aggregate(mv_2, bn_2)
                    more = first and not (isinstance(g, int) and g == CHUNKS - 1)
                    if more:
                        residual_scales(g + 1)
                    if first:
                        if par == 1:
                            dve.tensor_copy(lnT[:, :, 0:1], lnT[:, :, CHUNK:CHUNK + 1]).then_inc(prev_done, 1)
                        else:
                            dve.memset(lnT[:, :, 0:1], 0.0).then_inc(prev_done, 1)
                        dve.wait_ge(rstd_2_done, g + 1)
                        for t in range(NT):
                            dve.tensor_scalar(y[:, t, :], x2[par][:, t, :], mv_2[:, t, 0:1], rstd_2[:, t:t + 1],
                                              ALU.subtract, ALU.mult).then_inc(ln2_done, 1)
                    if more:
                        split_o(g + 1)
                    if first:
                        mix(g, "k")
                    if second:
                        gated(f, 0)
                    if first:
                        mix_lo(g, "k")
                    if second:
                        gated(f, 1)
                    if first:
                        mix(g, "r")
                    if second:
                        gated(f, 2)
                    if first:
                        mix_lo(g, "r")
                    if second:
                        gated(f, 3)

                over_steps(dve, step)

            @block.scalar
            def _(act):
                for i, n in enumerate(("r", "k", "v")):
                    for kc in range(KC):
                        u = KC * i + kc
                        act.wait_ge(w_turned, u + 1)
                        act.activation(hi[n][:, kc, :], bank[u % 8][:, :], ACT.Copy).then_inc(w_hi_done, 1)

                def split_o(g):
                    act.wait_ge(o_in, 16 * g + 16)
                    act.activation(o_hi[:, :, :], o_raw[:, :, :], ACT.Copy).then_inc(o_hi_done, 1)

                def mix_before(g, n, kc):
                    act.activation(mixed[:, kc, :], lnT[:, kc, 0:CHUNK], ACT.Copy,
                                   scale=mu1[n][:, kc:kc + 1]).then_inc(before_done[n], 1)

                def mix_hi(g, n, kc):
                    act.wait_ge(mixed_done[n], 4 * g + kc + 1)
                    act.activation(m_hi[n][:, kc, :], mixed[:, kc, :], ACT.Copy).then_inc(m_hi_done[n], 1)

                act.wait_ge(wo_split, 2)
                split_o(0)

                def step(g, par, first, second):
                    f = g - 1
                    if first:
                        act.wait_ge(x_in, 16 * g + 16)
                        act.wait_ge(xs_done, g + 1)
                        for t in range(NT):
                            act.activation(xc[:, t, :], xc[:, t, :], ACT.Identity, scale=xs[:, t, 0:1],
                                           bias=xs[:, t, 1:2]).then_inc(res_act, 1)
                    if second:
                        for d in range(KC):
                            act.wait_ge(k_done, 4 * f + d + 1)
                            if d >= 2:
                                act.wait_ge(act_lo_done, 4 * f + d - 1)
                            act.activation(relu[:, d % 2, :], ps_k[d % 2][:, :], ACT.Relu).then_inc(relu_done, 1)
                            act.wait_ge(relu_done, 4 * f + d + 1)
                            act.activation(act_hi[:, d, :], relu[:, d % 2, :], ACT.Square).then_inc(act_hi_done, 1)
                    if first and not (isinstance(g, int) and g == CHUNKS - 1):
                        act.wait_ge(y_done, 4 * g + 4)
                        split_o(g + 1)
                    if second:
                        for t in range(NT):
                            act.wait_ge(r_done, 4 * f + t + 1)
                            if not (isinstance(g, int) and g == 1):
                                act.wait_ge(out_done, 64 * f)
                            act.activation(gate[:, t, :], ps_r[t % 2][:, :], ACT.Sigmoid).then_inc(gate_done, 1)
                    if first:
                        for t in range(NT):
                            act.wait_ge(ln2_turned, 4 * g + t + 1)
                            if t == 0:
                                act.wait_ge(prev_done, g + 1)
                            act.activation(lnT[:, :, 1 + t * P:1 + (t + 1) * P],
                                           ps_y[t % 2][:, :].rearrange("p (k n) -> p k n", k=KC),
                                           ACT.Copy).then_inc(lnT_done, 1)
                        act.wait_ge(lnT_done, 4 * g + 4)
                        for kc in range(KC):
                            mix_before(g, "k", kc)
                        for kc in range(KC):
                            mix_hi(g, "k", kc)
                        for kc in range(KC):
                            act.wait_ge(m_lo_done["k"], 4 * g + kc + 1)
                            mix_before(g, "r", kc)
                        for kc in range(KC):
                            mix_hi(g, "r", kc)

                over_steps(act, step)

            @block.tensor
            def _(pe):
                for i, n in enumerate(("r", "k", "v")):
                    pe.wait_ge(w_in[i + 1], 16)
                    for kc in range(KC):
                        u = KC * i + kc
                        if u >= 8:
                            pe.wait_ge(w_lo_done, u - 7)
                        for d in range(KC):
                            ins = pe.transpose(bank[u % 8][:, d * P:(d + 1) * P], raw[n][:, d, kc * P:(kc + 1) * P],
                                               ident[:, :])
                        ins.then_inc(w_turned, 1)
                pe.wait_ge(w_lo_done, 3 * KC)

                def product(out, a_hi, a_lo, b_hi, b_lo, a_cols, b_cols, done):
                    prods = [(a, b, kc) for kc in range(KC) for a, b in ((a_lo, b_hi), (a_hi, b_lo), (a_hi, b_hi))]
                    for i, (a, b, kc) in enumerate(prods):
                        ins = pe.matmul(out, a[:, kc, a_cols], b[:, kc, b_cols], start=(i == 0), stop=(i == len(prods) - 1))
                    ins.then_inc(done, 1)

                whole = slice(0, C)

                def step(g, par, first, second):
                    f = g - 1
                    if first:
                        pe.wait_ge(o_hi_done, g + 1)
                        pe.wait_ge(o_lo_done, g + 1)
                        for t in range(NT):
                            if t < 2 and second:
                                pe.wait_ge(lnT_done, 4 * g - 1 + t)
                            if t >= 2:
                                pe.wait_ge(y_stored, 4 * g + t - 1)
                            product(ps_y[t % 2][:, :], o_hi, o_lo, hi["out"], lo["out"], slice(t * P, (t + 1) * P), whole, y_done)
                    if second:
                        pe.wait_ge(m_hi_done["k"], 4 * f + 4)
                        pe.wait_ge(m_lo_done["k"], 4 * f + 4)
                        for d in range(KC):
                            if d >= 2:
                                pe.wait_ge(relu_done, 4 * f + d - 1)
                            product(ps_k[d % 2][:, :], hi["k"], lo["k"], m_hi["k"], m_lo["k"], slice(d * P, (d + 1) * P), whole, k_done)
                        pe.wait_ge(m_hi_done["r"], 4 * f + 4)
                        pe.wait_ge(m_lo_done["r"], 4 * f + 4)
                        for t in range(NT):
                            if t >= 2:
                                pe.wait_ge(gate_done, 4 * f + t - 1)
                            product(ps_r[t % 2][:, :], m_hi["r"], m_lo["r"], hi["r"], lo["r"], slice(t * P, (t + 1) * P), whole, r_done)
                    if first:
                        for t in range(NT):
                            pe.wait_ge(ln2_done, 4 * g + t + 1)
                            if t < 2:
                                pe.wait_ge(y_stored, 4 * g + t + 3)
                            else:
                                pe.wait_ge(lnT_done, 4 * g + t - 1)
                            for k in range(KC):
                                ins = pe.transpose(ps_y[t % 2][:, k * P:(k + 1) * P], y[:, t, k * P:(k + 1) * P], ident[:, :])
                            ins.then_inc(ln2_turned, 1)
                    if second:
                        pe.wait_ge(act_lo_done, 4 * f + 4)
                        for t in range(NT):
                            if t >= 2:
                                pe.wait_ge(rkv_done, 4 * f + t - 1)
                            product(ps_v[t % 2][:, :], act_hi, act_lo, hi["v"], lo["v"], slice(t * P, (t + 1) * P), whole, kv_done)

                over_steps(pe, step)


def seq_preln_block(nc, x, w_qk, b_qk, w_v, b_v, w_out, b_out, gamma, beta, w_r, w_k, w_v2, mu_r, mu_k, out):
    with ExitStack() as ctx:
        ident = ctx.enter_context(nc.sbuf_tensor("ident", [P, P], F32))
        ln1_stats = ctx.enter_context(nc.sbuf_tensor("ln1_stats", [P, B * TT, 2], F32))
        o_scratch = nc.dram_tensor("o_scratch", [B, 2, HEADS, DH, HALF], F32, kind="Internal").ap()
        attention_pass(nc, x, w_qk, b_qk, w_v, b_v, o_scratch, ln1_stats, ident)
        mix_pass(nc, x, o_scratch, w_out, b_out, gamma, beta, w_r, w_k, w_v2, mu_r, mu_k, out, ln1_stats, ident)


_INS = ["L0_attn_x", "L0_attn_W_qk", "L0_attn_b_qk", "L0_attn_W_v", "L0_attn_b_v", "L0_attn_W_out", "L0_attn_b_out",
        "L0_attn_ln_gamma", "L0_attn_ln_beta", "L0_ffn_W_r", "L0_ffn_W_k", "L0_ffn_W_v", "L0_ffn_mu_r", "L0_ffn_mu_k"]


def kernel(**inputs):
    import numpy as _np
    import concourse.bacc as _bacc
    from concourse import mybir as _mybir
    from concourse.bass_utils import run_bass_kernel_spmd as _run

    nc = _bacc.Bacc("TRN2", target_bir_lowering=False, num_devices=1)
    arrays, args = {}, []
    for name in _INS:
        a = _np.ascontiguousarray(inputs[name])
        arrays[f"in_{name}_dram"] = a
        args.append(nc.dram_tensor(f"in_{name}_dram", a.shape, _mybir.dt.from_np(a.dtype), kind="ExternalInput").ap())
    args.append(nc.dram_tensor("out_dram", [B, T, C], F32, kind="ExternalOutput").ap())
    seq_preln_block(nc, *args)
    r = _run(nc, [arrays], core_ids=[0])
    return r.results[0]["out_dram"]
```

```python
from contextlib import ExitStack

import concourse.bass as bass
from concourse import mybir

F32 = mybir.dt.float32
F32R = mybir.dt.float32r
ALU = mybir.AluOpType
ACT = mybir.ActivationFunctionType
AX_X = mybir.AxisListType.X

P = 128
B, T, C = 8, 1024, 512
HEADS, DH = 8, 64
KC = C // P
TT = T // P
HALF = T // 2
SLOTS = HEADS * TT
LAST_SLOT = SLOTS + 6
XHAT_TURNS = [54, 55, 56, 57, 61, 62, 63, 64]
V_SLOTS = [0, 0, 1, 1, 2, 3, 4, 5]
QK_STORES = [2, 5]
NEXT_QK_STORES = [60, 66]
STATS_SLOT = 38
QUAD = 4
EPS = 1e-5
RSQRT2 = 2.0 ** -0.5
SCALE = DH ** -0.5


def f32(ap):
    return ap.bitcast(F32)


def query_tile(r):
    return r // 2 + (TT // 2) * (r % 2)


def attention_pass(nc, x, w_qk, b_qk, w_v, b_v, o_scratch, ln1_stats, ident):
    with ExitStack() as ctx:
        def sb(name, shape, dt=F32):
            return ctx.enter_context(nc.sbuf_tensor(name, shape, dt))

        def sem(name):
            return ctx.enter_context(nc.semaphore(name))

        wqk_hi = sb("wqk_hi", [P, KC, HEADS, 2, DH], F32R)
        wqk_lo = sb("wqk_lo", [P, KC, HEADS, 2, DH], F32R)
        wv_hi = sb("wv_hi", [P, KC, C], F32R)
        wv_lo = sb("wv_lo", [P, KC, C], F32R)
        bqk = sb("bqk", [P, HEADS])
        bv = sb("bv", [P, C])
        xT_hi = sb("xT_hi", [P, KC, T], F32R)
        xT_lo = sb("xT_lo", [P, KC, T], F32R)
        q_hilo = [sb(f"q_hilo{i}", [P, T], F32R) for i in range(2)]
        k_hihi = [sb(f"k_hihi{i}", [P, T], F32R) for i in range(2)]
        k_lolo = [sb(f"k_lolo{i}", [P, T], F32R) for i in range(2)]
        v = sb("v", [P, TT, C])
        probs = [sb(f"probs{i}", [P, T]) for i in range(3)]
        probsT = sb("probsT", [P, 2, TT, 2, 2 * P])
        neg_max = sb("neg_max", [P, 2, TT])
        row_sum = sb("row_sum", [P, 2, TT])
        row_inv = sb("row_inv", [P, 2, TT])
        inv_wide = sb("inv_wide", [P, 2, TT, DH])
        inv_cols = sb("inv_cols", [P, HALF])
        oT = [sb(f"oT{i}", [P, HALF]) for i in range(2)]
        xb = sb("xb", [P, TT, C])
        xhat = [sb(f"xhat{i}", [P, C]) for i in range(2)]
        bn6 = sb("bn6", [P, TT, 6])
        mean_var = sb("mean_var", [P, TT, 2])
        rstd = sb("rstd", [P, TT])
        neg_half = sb("neg_half", [P, TT])
        eps = sb("eps", [P, TT])
        wqk_raw = probsT[:, 0].rearrange("p a b c -> p (a b c)").rearrange("p (k h d s) -> p k h d s", k=KC, h=HEADS, s=2)
        wv_raw = probsT[:, 1].rearrange("p a b c -> p (a b c)")[:, 0:KC * C].rearrange("p (k n) -> p k n", k=KC)

        ps_scores = [ctx.enter_context(nc.psum_tensor(f"ps_scores{i}", [P, T], F32)) for i in range(2)]
        ps_turnA = ctx.enter_context(nc.psum_tensor("ps_turnA", [P, 4, P], F32))
        ps_turnB = ctx.enter_context(nc.psum_tensor("ps_turnB", [P, 4, P], F32))
        ps_o = ctx.enter_context(nc.psum_tensor("ps_o", [P, HALF], F32))
        ps_misc = ctx.enter_context(nc.psum_tensor("ps_misc", [P, HALF], F32))
        v_banks = [ps_turnA[:, :, :].rearrange("p a b -> p (a b)"), ps_turnB[:, :, :].rearrange("p a b -> p (a b)")] * 2
        v_banks = v_banks[0:3] + [ps_o[:, :]] * 5
        misc4 = ps_misc[:, :].rearrange("p (k n) -> p k n", k=KC)
        first_turns = [misc4, ps_turnA[:, :, :], ps_turnB[:, :, :], ps_o[:, :].rearrange("p (k n) -> p k n", k=KC)]

        wqk_in = [sem(f"wqk_in{i}") for i in range(KC)]
        wv_in = sem("wv_in")
        b_in = sem("b_in")
        bqk_done = sem("bqk_done")
        wq_scaled = sem("wq_scaled")
        wq_hi_done = sem("wq_hi_done")
        wq_lo_done = sem("wq_lo_done")
        wk_hi_done = sem("wk_hi_done")
        wk_lo_done = sem("wk_lo_done")
        wv_hi_done = sem("wv_hi_done")
        wv_lo_done = sem("wv_lo_done")
        x_in = [sem(f"x_in{i}") for i in range(4)]
        bn_done = sem("bn_done")
        bn_step = sem("bn_step")
        eps_done = sem("eps_done")
        rstd_done = sem("rstd_done")
        half_set = sem("half_set")
        xhat_done = sem("xhat_done")
        xhatT_done = sem("xhatT_done")
        xT_hi_done = sem("xT_hi_done")
        xT_lo_done = sem("xT_lo_done")
        qk_done = sem("qk_done")
        qk_hi_done = sem("qk_hi_done")
        qk_lo_done = sem("qk_lo_done")
        k_copied = [sem(f"k_copied{i}") for i in range(2)]
        v_done = sem("v_done")
        v_stored = sem("v_stored")
        scores_done = sem("scores_done")
        max_done = sem("max_done")
        exp_done = sem("exp_done")
        turnA_done = sem("turnA_done")
        turnB_done = sem("turnB_done")
        turnA_stored = sem("turnA_stored")
        turnB_stored = sem("turnB_stored")
        pv_done = sem("pv_done")
        recip_done = sem("recip_done")
        inv_done = sem("inv_done")
        inv_turned = sem("inv_turned")
        inv_stored = sem("inv_stored")
        o_done = sem("o_done")
        oT_free = [sem(f"oT_free{i}") for i in range(2)]
        ident_set = sem("ident_set")
        stats_kept = sem("stats_kept")

        x_tiles = x.rearrange("b (t p) c -> b p t c", p=P)

        with nc.Block() as block:

            @block.sync
            def _(sp):
                def load_x(b, i):
                    sp.dma_start(xb[:, 2 * i:2 * i + 2, :], x_tiles[b][:, 2 * i:2 * i + 2, :]).then_inc(x_in[i], 16)

                for i in range(4):
                    load_x(0, i)
                wqk_view = w_qk.rearrange("(k p) (h d s) -> k p h d s", p=P, h=HEADS, s=2)
                for kc in range(KC):
                    sp.dma_start(wqk_raw[:, kc], wqk_view[kc]).then_inc(wqk_in[kc], 16)
                bqk_view = b_qk.rearrange("(h d s) -> s d h", h=HEADS, s=2)
                for s in range(2):
                    sp.dma_start(bqk[s * DH:(s + 1) * DH, :], bqk_view[s], allow_slow_non_contiguous=True).then_inc(b_in, 16)
                sp.dma_start(wv_raw, w_v.rearrange("(k p) n -> p k n", p=P)).then_inc(wv_in, 16)
                sp.dma_start(bv[:, :], b_v.rearrange("(o n) -> o n", o=1).broadcast_to([P, C])).then_inc(b_in, 16)

                def copy_k(b, h):
                    sp.wait_ge(qk_lo_done, 16 * b + 2 * h + 2)
                    sp.dma_start(f32(k_hihi[h % 2][0:DH, :]), f32(k_hihi[h % 2][DH:P, :])).then_inc(k_copied[h % 2], 16)
                    sp.dma_start(f32(k_lolo[h % 2][0:DH, :]), f32(k_lolo[h % 2][DH:P, :])).then_inc(k_copied[h % 2], 16)

                def store_o(b, h):
                    sp.wait_ge(o_done, 8 * b + h + 1)
                    for half in range(2):
                        sp.dma_start(o_scratch[b][half, h, :, :],
                                     oT[h % 2][half * DH:(half + 1) * DH, :]).then_inc(oT_free[h % 2], 16)

                copy_k(0, 0)

                def entry(b, last):
                    for h in range(HEADS + 1):
                        if h == 0 and not last:
                            sp.wait_ge(xhat_done, 8 * b + 8)
                        if h < 4 and not last:
                            load_x(b + 1, h)
                        if h < HEADS - 1:
                            copy_k(b, h + 1)
                        if h == HEADS and not last:
                            copy_k(b + 1, 0)
                        if h >= 1:
                            store_o(b, h - 1)

                with sp.Fori(0, B - 1) as b:
                    entry(b, False)
                entry(B - 1, True)
                for i in range(2):
                    sp.wait_ge(oT_free[i], 16 + 128 * B)

            @block.gpsimd
            def _(pool):
                pool.memset(ident[:, :], 0.0).then_inc(ident_set, 1)
                pool.wait_ge(ident_set, 1)
                pool.affine_select(out=ident[:, :], in_=ident[:, :], compare_op=ALU.not_equal, fill=1.0, base=0,
                                   pattern=[[-1, P]], channel_multiplier=1).then_inc(ident_set, 1)
                pool.memset(neg_half[:, :], -0.5).then_inc(half_set, 1)
                pool.memset(eps[:, :], EPS).then_inc(half_set, 1)
                pool.wait_ge(half_set, 2)

                def rstd_of(b):
                    pool.wait_ge(bn_done, b + 1)
                    pool.tensor_tensor(rstd[:, :], mean_var[:, :, 1], eps[:, :], ALU.add).then_inc(eps_done, 1)
                    pool.wait_ge(eps_done, b + 1)
                    pool.tensor_tensor(rstd[:, :], rstd[:, :], neg_half[:, :], ALU.pow).then_inc(rstd_done, 1)

                rstd_of(0)
                for kc in range(KC):
                    pool.wait_ge(wk_hi_done, kc + 1)
                    pool.tensor_tensor(wqk_lo[:, kc, :, 1, :], wqk_raw[:, kc, :, :, 1], f32(wqk_hi[:, kc, :, 1, :]),
                                       ALU.subtract).then_inc(wk_lo_done, 1)
                pool.wait_ge(wv_hi_done, 1)
                pool.tensor_tensor(wv_lo[:, :, :], wv_raw, f32(wv_hi[:, :, :]), ALU.subtract).then_inc(wv_lo_done, 1)
                with pool.Fori(0, B - 1) as b:
                    rstd_of(b + 1)

            @block.vector
            def _(dve):
                for i in range(2):
                    dve.memset(oT[i][:, :], 0.0).then_inc(oT_free[i], 16)
                def stats(b, t):
                    dve.wait_ge(x_in[t // 2], 16 * b + 16)
                    dve.bn_stats(bn6[:, t, :], xb[:, t, :]).then_inc(bn_step, 1)

                def aggregate():
                    for t in range(TT):
                        ins = dve.bn_aggr(mean_var[:, t, :], bn6[:, t, :])
                    ins.then_inc(bn_done, 1)

                def keep_stats(b):
                    dve.wait_ge(rstd_done, b + 1)
                    dve.tensor_copy(ln1_stats[:, bass.ds(b * TT, TT), 0], mean_var[:, :, 0])
                    dve.tensor_copy(ln1_stats[:, bass.ds(b * TT, TT), 1], rstd[:, :]).then_inc(stats_kept, 1)

                def normalise(b, t):
                    if t >= 2:
                        dve.wait_ge(xhatT_done, 8 * b + t - 1)
                    dve.tensor_scalar(xhat[t % 2][:, :], xb[:, t, :], mean_var[:, t, 0:1], rstd[:, t:t + 1],
                                      ALU.subtract, ALU.mult).then_inc(xhat_done, 1)

                def store_xT_lo(b, t, turned):
                    dve.wait_ge(xT_hi_done, 8 * b + t + 1)
                    cols = slice(t * P, (t + 1) * P)
                    dve.tensor_tensor(xT_lo[:, :, cols], turned, f32(xT_hi[:, :, cols]),
                                      ALU.subtract).then_inc(xT_lo_done, 1)

                def store_qk_lo(b, h, half, ps=ps_misc):
                    dve.wait_ge(qk_hi_done, 16 * b + 2 * h + half + 1)
                    cols = slice(half * HALF, (half + 1) * HALF)
                    i = h % 2
                    dve.scalar_tensor_tensor(q_hilo[i][DH:P, cols], ps[0:DH, :], bqk[0:DH, h:h + 1],
                                             f32(q_hilo[i][0:DH, cols]), ALU.add, ALU.subtract)
                    dve.scalar_tensor_tensor(k_lolo[i][DH:P, cols], ps[DH:P, :], bqk[DH:P, h:h + 1],
                                             f32(k_hihi[i][DH:P, cols]), ALU.add, ALU.subtract).then_inc(qk_lo_done, 1)

                for t in range(TT):
                    stats(0, t)
                dve.wait_ge(bn_step, TT)
                aggregate()
                keep_stats(0)
                for t in range(TT):
                    normalise(0, t)
                    if t >= 2:
                        store_xT_lo(0, t - 2, first_turns[(t - 2) % 4])
                dve.wait_ge(b_in, 48)
                dve.tensor_scalar(bqk[0:DH, :], bqk[0:DH, :], SCALE, None, ALU.mult).then_inc(bqk_done, 1)
                for t in (TT - 2, TT - 1):
                    store_xT_lo(0, t, first_turns[t % 4])
                for kc in range(KC):
                    dve.wait_ge(wq_hi_done, kc + 1)
                    dve.tensor_tensor(wqk_lo[:, kc, :, 0, :], wqk_raw[:, kc, :, :, 0], f32(wqk_hi[:, kc, :, 0, :]),
                                      ALU.subtract).then_inc(wq_lo_done, 1)
                for half in range(2):
                    store_qk_lo(0, 0, half, (ps_misc, ps_o)[half])

                def entry(b, last):
                    for n in range(LAST_SLOT):
                        h, r = n // TT, n % TT
                        if n == STATS_SLOT + TT and not last:
                            dve.wait_ge(bn_step, 8 * b + 16)
                        if n < SLOTS:
                            dve.wait_ge(scores_done, 64 * b + n + 1)
                            dve.tensor_reduce(neg_max[:, h % 2, r:r + 1], ps_scores[n % 2][:, :], AX_X, ALU.max,
                                              negate=True).then_inc(max_done, 1)
                        for t in range(TT):
                            if V_SLOTS[t] == n:
                                dve.wait_ge(v_done, 8 * b + t + 1)
                                dve.tensor_tensor(v[:, t, :], v_banks[t], bv[:, :], ALU.add).then_inc(v_stored, 1)
                        if r == 1 and h >= 1:
                            dve.wait_ge(exp_done, 64 * b + 8 * h)
                            dve.reciprocal(row_inv[:, (h - 1) % 2, :], row_sum[:, (h - 1) % 2, :]).then_inc(recip_done, 1)
                            dve.wait_ge(recip_done, 8 * b + h)
                            dve.tensor_copy(inv_wide[:, (h - 1) % 2, :, :],
                                            row_inv[:, (h - 1) % 2, :].unsqueeze(2).broadcast_to([P, TT, DH])).then_inc(inv_done, 1)
                        if r in QK_STORES and h < HEADS - 1:
                            store_qk_lo(b, h + 1, QK_STORES.index(r))
                        if n in NEXT_QK_STORES and not last:
                            store_qk_lo(b + 1, 0, NEXT_QK_STORES.index(n))
                        if not last:
                            if STATS_SLOT <= n < STATS_SLOT + TT:
                                stats(b + 1, n - STATS_SLOT)
                            if n == STATS_SLOT + TT:
                                aggregate()
                            if n == XHAT_TURNS[0] - 3:
                                keep_stats(b + 1)
                            if XHAT_TURNS[0] - 2 <= n < XHAT_TURNS[0]:
                                normalise(b + 1, n - XHAT_TURNS[0] + 2)
                            if n - 1 in XHAT_TURNS:
                                store_xT_lo(b + 1, XHAT_TURNS.index(n - 1), misc4)
                        if 2 <= n < SLOTS + 2:
                            m = n - 2
                            dve.wait_ge(turnB_done, 64 * b + m + 1)
                            dve.tensor_copy(probsT[:, m // QUAD % 2, 4:8, m % 2, m % QUAD // 2 * P:(m % QUAD // 2 + 1) * P],
                                            ps_turnB[:, :, :]).then_inc(turnB_stored, 1)
                        if not last and n - 1 in XHAT_TURNS[:-2]:
                            normalise(b + 1, XHAT_TURNS.index(n - 1) + 2)
                        if r == 5 and h >= 1:
                            dve.wait_ge(pv_done, 8 * b + h)
                            dve.wait_ge(inv_stored, 8 * b + h)
                            dve.wait_ge(oT_free[(h - 1) % 2], 128 * b + 16 + 32 * ((h - 1) // 2))
                            dve.tensor_tensor(oT[(h - 1) % 2][:, :], ps_o[:, :], inv_cols[:, :],
                                              ALU.mult).then_inc(o_done, 1)

                with dve.Fori(0, B - 1) as b:
                    entry(b, False)
                entry(B - 1, True)

            @block.scalar
            def _(act):
                def split_wqk(kc):
                    act.wait_ge(wqk_in[kc], 16)
                    act.activation(wqk_hi[:, kc, :, 1, :], wqk_raw[:, kc, :, :, 1], ACT.Copy).then_inc(wk_hi_done, 1)
                    act.activation(wqk_raw[:, kc, :, :, 0], wqk_raw[:, kc, :, :, 0], ACT.Copy,
                                   scale=SCALE).then_inc(wq_scaled, 1)
                    act.wait_ge(wq_scaled, kc + 1)
                    act.activation(wqk_hi[:, kc, :, 0, :], wqk_raw[:, kc, :, :, 0], ACT.Copy).then_inc(wq_hi_done, 1)

                def store_xT_hi(b, t, turned):
                    act.wait_ge(xhatT_done, 8 * b + t + 1)
                    act.activation(xT_hi[:, :, t * P:(t + 1) * P], turned, ACT.Copy).then_inc(xT_hi_done, 1)

                def store_qk_hi(b, h, half, ps=ps_misc):
                    act.wait_ge(qk_done, 16 * b + 2 * h + half + 1)
                    cols = slice(half * HALF, (half + 1) * HALF)
                    i = h % 2
                    act.activation(q_hilo[i][0:DH, cols], ps[0:DH, :], ACT.Identity, bias=bqk[0:DH, h:h + 1])
                    act.activation(k_hihi[i][DH:P, cols], ps[DH:P, :], ACT.Identity,
                                   bias=bqk[DH:P, h:h + 1]).then_inc(qk_hi_done, 1)

                def store_inv(b, h):
                    act.wait_ge(inv_turned, 8 * b + h)
                    if h >= 2:
                        act.wait_ge(o_done, 8 * b + h - 1)
                    act.activation(inv_cols[:, :], ps_misc[:, :], ACT.Copy).then_inc(inv_stored, 1)

                for kc in range(KC - 1):
                    split_wqk(kc)
                for t in range(TT):
                    store_xT_hi(0, t, first_turns[t % 4])
                    if t == 1:
                        split_wqk(KC - 1)
                act.wait_ge(wv_in, 16)
                act.activation(wv_hi[:, :, :], wv_raw, ACT.Copy).then_inc(wv_hi_done, 1)
                act.wait_ge(bqk_done, 1)
                for half in range(2):
                    store_qk_hi(0, 0, half, (ps_misc, ps_o)[half])

                def entry(b, last):
                    for n in range(LAST_SLOT):
                        h, r = n // TT, n % TT
                        if 1 <= n <= SLOTS:
                            m = n - 1
                            act.wait_ge(max_done, 64 * b + m + 1)
                            if m >= 3:
                                act.wait_ge(turnB_done, 64 * b + m - 2)
                            act.activation(probs[m % 3][:, :], ps_scores[m % 2][:, :], ACT.Exp,
                                           bias=neg_max[:, m // TT % 2, m % TT:m % TT + 1],
                                           accum_out=row_sum[:, m // TT % 2, m % TT:m % TT + 1]).then_inc(exp_done, 1)
                        if n == 61:
                            store_inv(b, 7)
                        if r in QK_STORES and h < HEADS - 1:
                            store_qk_hi(b, h + 1, QK_STORES.index(r))
                        if n in NEXT_QK_STORES and not last:
                            store_qk_hi(b + 1, 0, NEXT_QK_STORES.index(n))
                        if not last and n - 1 in XHAT_TURNS:
                            store_xT_hi(b + 1, XHAT_TURNS.index(n - 1), misc4)
                        if 2 <= n < SLOTS + 2:
                            m = n - 2
                            act.wait_ge(turnA_done, 64 * b + m + 1)
                            act.activation(probsT[:, m // QUAD % 2, 0:4, m % 2, m % QUAD // 2 * P:(m % QUAD // 2 + 1) * P],
                                           ps_turnA[:, :, :], ACT.Copy).then_inc(turnA_stored, 1)
                        if r == 3 and h >= 1 and h != HEADS - 1:
                            store_inv(b, h)

                with act.Fori(0, B - 1) as b:
                    entry(b, False)
                entry(B - 1, True)

            @block.tensor
            def _(pe):
                def turn_xhat(b, t, turned):
                    pe.wait_ge(xhat_done, 8 * b + t + 1)
                    for k in range(KC):
                        ins = pe.transpose(turned[:, k, :], xhat[t % 2][:, k * P:(k + 1) * P], ident[:, :])
                    ins.then_inc(xhatT_done, 1)

                def project_qk(b, h, half, first, end, ps=ps_misc):
                    cols = slice(half * HALF, (half + 1) * HALF)
                    prods = [(w, xt, kc) for kc in range(KC) for w, xt in ((wqk_lo, xT_hi), (wqk_hi, xT_lo), (wqk_hi, xT_hi))]
                    for n in range(first, end):
                        w, xt, kc = prods[n]
                        ins = pe.matmul(ps[:, :], w[:, kc, h, :, :].rearrange("p s d -> p (s d)"), xt[:, kc, cols],
                                        start=(n == 0), stop=(n == 11))
                    if end == 12:
                        ins.then_inc(qk_done, 1)

                def misc_free_of_qk(b, h, half):
                    pe.wait_ge(qk_hi_done, 16 * b + 2 * h + half + 1)
                    pe.wait_ge(qk_lo_done, 16 * b + 2 * h + half + 1)

                def misc_free_of_xhat(b, t):
                    pe.wait_ge(xT_hi_done, 8 * b + t + 1)
                    pe.wait_ge(xT_lo_done, 8 * b + t + 1)

                pe.wait_ge(ident_set, 2)
                for t in range(TT):
                    if t >= 4:
                        misc_free_of_xhat(0, t - 4)
                    turn_xhat(0, t, first_turns[t % 4])
                misc_free_of_xhat(0, TT - 1)
                pe.wait_ge(wk_lo_done, KC)
                pe.wait_ge(wq_lo_done, KC)
                for half in range(2):
                    project_qk(0, 0, half, 0, 12, (ps_misc, ps_o)[half])
                pe.wait_ge(wv_lo_done, 1)

                def project_v(b, t):
                    prods = [(xt, w, kc) for kc in range(KC) for xt, w in ((xT_lo, wv_hi), (xT_hi, wv_lo), (xT_hi, wv_hi))]
                    for i, (xt, w, kc) in enumerate(prods):
                        ins = pe.matmul(v_banks[t], xt[:, kc, t * P:(t + 1) * P], w[:, kc, :], start=(i == 0), stop=(i == 11))
                    ins.then_inc(v_done, 1)

                def scores(b, n):
                    h, r = n // TT, n % TT
                    if r == 0:
                        pe.wait_ge(qk_lo_done, 16 * b + 2 * h + 2)
                        pe.wait_ge(k_copied[h % 2], 128 * b + 32 * (h // 2) + 32)
                    if n >= 2:
                        pe.wait_ge(exp_done, 64 * b + n - 1)
                    tile = slice(query_tile(r) * P, (query_tile(r) + 1) * P)
                    for half in range(2):
                        cols = slice(half * HALF, (half + 1) * HALF)
                        for i, k in enumerate((k_lolo, k_hihi)):
                            ins = pe.matmul(ps_scores[n % 2][:, cols], q_hilo[h % 2][:, tile], k[h % 2][:, cols],
                                            start=(i == 0), stop=(i == 1))
                    ins.then_inc(scores_done, 1)

                def turn_probs(b, m):
                    pe.wait_ge(exp_done, 64 * b + m + 1)
                    for ps, first, stored, done in ((ps_turnA, 0, turnA_stored, turnA_done),
                                                    (ps_turnB, 4, turnB_stored, turnB_done)):
                        if m >= 1:
                            pe.wait_ge(stored, 64 * b + m)
                        for j in range(4):
                            ins = pe.transpose(ps[:, j, :], probs[m % 3][:, (first + j) * P:(first + j + 1) * P], ident[:, :])
                        ins.then_inc(done, 1)

                def p_at_v(b, quad, part):
                    h, q2 = quad // 2, quad % 2
                    if part == 0:
                        pe.wait_ge(turnA_stored, 64 * b + QUAD * quad + QUAD)
                        pe.wait_ge(turnB_stored, 64 * b + QUAD * quad + QUAD)
                        if q2 == 0 and h >= 1:
                            pe.wait_ge(o_done, 8 * b + h)
                    for jt in (2 * part, 2 * part + 1):
                        for half in range(2):
                            ins = pe.matmul(ps_o[half * DH:(half + 1) * DH, q2 * 2 * P:(q2 + 1) * 2 * P],
                                            v[:, jt, h * DH:(h + 1) * DH], probsT[:, quad % 2, jt, half, :],
                                            start=(jt == 0), stop=(jt == TT - 1))
                    if part == 3 and q2 == 1:
                        ins.then_inc(pv_done, 1)

                def spread_inv(b, h):
                    pe.wait_ge(inv_done, 8 * b + h + 1)
                    for m in range(4):
                        cols = inv_wide[:, h % 2, 2 * m:2 * m + 2, :].rearrange("p r d -> p (r d)")
                        ins = pe.transpose(ps_misc[:, m * P:(m + 1) * P], cols, ident[:, :])
                    ins.then_inc(inv_turned, 1)

                def entry(b, last):
                    for n in range(LAST_SLOT):
                        h, r = n // TT, n % TT
                        if n < SLOTS:
                            scores(b, n)
                        for t in range(TT):
                            if V_SLOTS[t] == n:
                                if t in (2, 4, 5, 6, 7):
                                    pe.wait_ge(v_stored, 8 * b + (1 if t == 2 else t))
                                project_v(b, t)
                        if r == 3 and 1 <= h < HEADS - 1:
                            misc_free_of_qk(b, h + 1, 0)
                            spread_inv(b, h - 1)
                        if n == SLOTS + 3:
                            if not last:
                                misc_free_of_qk(b + 1, 0, 1)
                            spread_inv(b, HEADS - 1)
                        if n == 2:
                            pe.wait_ge(v_stored, 8 * b + 3)
                        if 2 <= n < SLOTS + 2:
                            turn_probs(b, n - 2)
                        if n == 6:
                            pe.wait_ge(v_stored, 8 * b + TT)
                        if n >= 6:
                            p_at_v(b, (n - 6) // QUAD, (n - 6) % QUAD)
                        if h < HEADS - 1:
                            if n == 0:
                                misc_free_of_qk(b, 0, 1)
                                project_qk(b, 1, 0, 0, 4)
                            if r == 0:
                                project_qk(b, h + 1, 0, 4, 8)
                            if r == 1:
                                project_qk(b, h + 1, 0, 8, 12)
                            if r == 3:
                                misc_free_of_qk(b, h + 1, 0)
                                if h >= 1:
                                    pe.wait_ge(inv_stored, 8 * b + h)
                                project_qk(b, h + 1, 1, 0, 6)
                            if r == 4:
                                project_qk(b, h + 1, 1, 6, 12)
                            if r == 7 and h < HEADS - 2:
                                misc_free_of_qk(b, h + 1, 1)
                                project_qk(b, h + 2, 0, 0, 4)
                        if n == 60:
                            if last:
                                misc_free_of_qk(b, h, 1)
                            else:
                                misc_free_of_qk(b + 1, 0, 0)
                            spread_inv(b, h - 1)
                        if not last:
                            if n in XHAT_TURNS:
                                t = XHAT_TURNS.index(n)
                                if t == 0:
                                    misc_free_of_qk(b, HEADS - 1, 1)
                                elif t == 4:
                                    pe.wait_ge(inv_stored, 8 * b + h)
                                else:
                                    misc_free_of_xhat(b + 1, t - 1)
                                turn_xhat(b + 1, t, misc4)
                            if n == 58:
                                misc_free_of_xhat(b + 1, 3)
                                project_qk(b + 1, 0, 0, 0, 6)
                            if n == 59:
                                project_qk(b + 1, 0, 0, 6, 12)
                            if n == 65:
                                misc_free_of_xhat(b + 1, TT - 1)
                                project_qk(b + 1, 0, 1, 0, 12)
                            if n == LAST_SLOT - 1:
                                pe.wait_ge(inv_stored, 8 * b + HEADS)

                with pe.Fori(0, B - 1) as b:
                    entry(b, False)
                entry(B - 1, True)


def mix_pass(nc, x, o_scratch, w_out, b_out, gamma, beta, w_r, w_k, w_v, mu_r, mu_k, out, ln1_stats, ident):
    with ExitStack() as ctx:
        def sb(name, shape, dt=F32):
            return ctx.enter_context(nc.sbuf_tensor(name, shape, dt))

        def sem(name):
            return ctx.enter_context(nc.semaphore(name))

        CHUNK = T // 2
        NT = CHUNK // P
        CHUNKS = B * 2
        NAMES = ("out", "r", "k", "v")

        hi = {n: sb(f"mix_w{n}_hi", [P, KC, C], F32R) for n in NAMES}
        lo = {n: sb(f"mix_w{n}_lo", [P, KC, C], F32R) for n in NAMES}
        gam = sb("gam", [P, C])
        bet = sb("bet", [P, C])
        bo = sb("bo", [P, C])
        mu = {"k": sb("mu_k", [P, KC]), "r": sb("mu_r", [P, KC])}
        mu1 = {"k": sb("mu1_k", [P, KC]), "r": sb("mu1_r", [P, KC])}
        neg_half = sb("neg_half2", [P, NT])
        eps = sb("eps2", [P, NT])
        st1 = sb("st1", [P, NT, 2])
        xs = sb("xs", [P, NT, 2])
        o_raw = sb("o_raw", [P, KC, CHUNK])
        o_hi = sb("o_hi", [P, KC, CHUNK], F32R)
        o_lo = sb("o_lo", [P, KC, CHUNK], F32R)
        xc = sb("xc", [P, NT, C])
        y = sb("y", [P, NT, C])
        x2 = [sb(f"x2_{i}", [P, NT, C]) for i in range(2)]
        bn6 = sb("bn6b", [P, NT, 6])
        mv_y = sb("mv_y", [P, NT, 2])
        mv_2 = sb("mv_2", [P, NT, 2])
        rstd_y = sb("rstd_y", [P, NT])
        rstd_2 = sb("rstd_2", [P, NT])
        lnT = sb("lnT", [P, KC, CHUNK + 1])
        mixed = sb("mixed", [P, KC, CHUNK])
        m_hi = {n: sb(f"m{n}_hi", [P, KC, CHUNK], F32R) for n in "kr"}
        m_lo = {n: sb(f"m{n}_lo", [P, KC, CHUNK], F32R) for n in "kr"}
        relu = sb("relu", [P, 2, CHUNK])
        act_hi = sb("act_hi", [P, KC, CHUNK], F32R)
        act_lo = sb("act_lo", [P, KC, CHUNK], F32R)
        gate = sb("gate", [P, NT, C])
        raw = {"out": o_raw, "r": mixed, "k": y, "v": gate}

        bank = [ctx.enter_context(nc.psum_tensor(f"bank{i}", [P, C], F32)) for i in range(8)]
        ps_y, ps_k, ps_r, ps_v = bank[0:2], bank[2:4], bank[4:6], bank[6:8]

        w_in = [sem(f"wc_in{i}") for i in range(5)]
        small_set = sem("small_set")
        w_turned = sem("w_turned")
        w_hi_done = sem("w_hi_done")
        w_lo_done = sem("w_lo_done")
        wo_split = sem("wo_split")
        o_in = sem("o_in")
        x_in = sem("xc_in")
        o_hi_done = sem("o_hi_done")
        o_lo_done = sem("o_lo_done")
        y_done = sem("y_done")
        y_stored = sem("y_stored")
        bn_step = sem("bn_step2")
        bn_y = sem("bn_y")
        eps_step = sem("eps_step")
        rstd_y_done = sem("rstd_y_done")
        xs_step = sem("xs_step")
        xs_done = sem("xs_done")
        res_act = sem("res_act")
        res_done = sem("res_done")
        t1_done = sem("t1_done")
        x2_done = sem("x2_done")
        bn2_step = sem("bn2_step")
        bn_2 = sem("bn_2")
        rstd_2_done = sem("rstd_2_done")
        ln2_done = sem("ln2_done")
        ln2_turned = sem("ln2_turned")
        prev_done = sem("prev_done")
        lnT_done = sem("lnT_done")
        before_done = {n: sem(f"before_{n}") for n in "kr"}
        mixed_done = {n: sem(f"mixed_{n}") for n in "kr"}
        m_hi_done = {n: sem(f"m_hi_{n}") for n in "kr"}
        m_lo_done = {n: sem(f"m_lo_{n}") for n in "kr"}
        k_done = sem("k_done")
        relu_done = sem("relu_done")
        act_hi_done = sem("act_hi_done")
        sq_done = sem("sq_done")
        act_lo_done = sem("act_lo_done")
        r_done = sem("r_done")
        gate_done = sem("gate_done")
        kv_done = sem("kv_done")
        rkv_done = sem("rkv_done")
        sum_done = sem("sum_done")
        out_done = sem("out_done")

        o_view = o_scratch.rearrange("b c h d t -> (b c) (h d) t").rearrange("g (k p) t -> g p k t", p=P)
        x_view = x.rearrange("b (c t p) n -> (b c) p t n", c=2, p=P)
        out_view = out.rearrange("b (c t p) n -> (b c) p t n", c=2, p=P)

        def spread(vec):
            return vec.rearrange("(o n) -> o n", o=1).broadcast_to([P, C])

        def over_steps(eng, step):
            step(0, 0, True, False)
            with eng.Fori(0, CHUNKS // 2 - 1) as i:
                step(2 * i + 1, 1, True, True)
                step(2 * i + 2, 0, True, True)
            step(CHUNKS - 1, 1, True, True)
            step(CHUNKS, 0, False, True)

        with nc.Block() as block:

            @block.sync
            def _(sp):
                for i, (n, w) in enumerate((("out", w_out), ("r", w_r), ("k", w_k), ("v", w_v))):
                    sp.dma_start(raw[n][:, :, :], w.rearrange("(k p) n -> p k n", p=P)).then_inc(w_in[i], 16)
                for dst, src in ((gam, gamma), (bet, beta), (bo, b_out)):
                    sp.dma_start(dst[:, :], spread(src)).then_inc(w_in[4], 16)
                for dst, src in ((mu["k"], mu_k), (mu["r"], mu_r)):
                    sp.dma_start(dst[:, :], src.rearrange("(k p) -> p k", p=P),
                                 allow_slow_non_contiguous=True).then_inc(w_in[4], 16)

                def load_o(g):
                    sp.dma_start(o_raw[:, :, :], o_view[g]).then_inc(o_in, 16)

                def load_x(g):
                    sp.dma_start(xc[:, :, :], x_view[g]).then_inc(x_in, 16)

                sp.wait_ge(wo_split, 2)
                load_o(0)
                load_x(0)

                def step(g, par, first, second):
                    if first and not (isinstance(g, int) and g == CHUNKS - 1):
                        sp.wait_ge(o_lo_done, g + 1)
                        load_o(g + 1)
                        sp.wait_ge(x2_done, 4 * g + 4)
                        load_x(g + 1)
                    if second:
                        for t in range(NT):
                            sp.wait_ge(sum_done, 4 * g - 3 + t)
                            sp.dma_start(out_view[g - 1][:, t, :], gate[:, t, :]).then_inc(out_done, 16)

                over_steps(sp, step)
                sp.wait_ge(out_done, 16 * NT * CHUNKS)

            @block.gpsimd
            def _(pool):
                pool.memset(eps[:, :], EPS).then_inc(eps_step, 1)
                pool.memset(neg_half[:, :], -0.5).then_inc(eps_step, 1)
                pool.wait_ge(eps_step, 2)
                pool.wait_ge(small_set, 2)

                def step(g, par, first, second):
                    if first:
                        pool.wait_ge(bn_y, g + 1)
                        pool.tensor_tensor(rstd_y[:, :], mv_y[:, :, 1], eps[:, :], ALU.add).then_inc(eps_step, 1)
                        pool.wait_ge(eps_step, 2 * g + 3)
                        pool.tensor_tensor(rstd_y[:, :], rstd_y[:, :], neg_half[:, :], ALU.pow).then_inc(rstd_y_done, 1)
                        for t in range(NT):
                            pool.wait_ge(res_act, 4 * g + t + 1)
                            pool.tensor_tensor(xc[:, t, :], xc[:, t, :], bet[:, :], ALU.add).then_inc(res_done, 1)
                        pool.wait_ge(bn_2, g + 1)
                        pool.tensor_tensor(rstd_2[:, :], mv_2[:, :, 1], eps[:, :], ALU.add).then_inc(eps_step, 1)
                        pool.wait_ge(eps_step, 2 * g + 4)
                        pool.tensor_tensor(rstd_2[:, :], rstd_2[:, :], neg_half[:, :], ALU.pow).then_inc(rstd_2_done, 1)
                    if second:
                        for t in range(NT):
                            pool.wait_ge(rkv_done, 4 * g - 3 + t)
                            pool.tensor_tensor(gate[:, t, :], gate[:, t, :], x2[1 - par][:, t, :],
                                               ALU.add).then_inc(sum_done, 1)

                over_steps(pool, step)

            @block.vector
            def _(dve):
                dve.wait_ge(w_in[4], 80)
                dve.tensor_scalar(gam[:, :], gam[:, :], RSQRT2, None, ALU.mult).then_inc(small_set, 1)
                dve.tensor_scalar(bet[:, :], bet[:, :], RSQRT2, None, ALU.mult).then_inc(small_set, 1)
                for n in "kr":
                    dve.tensor_scalar(mu1[n][:, :], mu[n][:, :], -1.0, 1.0, ALU.mult, ALU.add).then_inc(small_set, 1)
                dve.memset(lnT[:, :, 0:1], 0.0).then_inc(small_set, 1)
                dve.wait_ge(w_in[0], 16)
                dve.tensor_copy(hi["out"][:, :, :], raw["out"][:, :, :]).then_inc(wo_split, 1)
                dve.wait_ge(wo_split, 1)
                dve.tensor_tensor(lo["out"][:, :, :], raw["out"][:, :, :], f32(hi["out"][:, :, :]),
                                  ALU.subtract).then_inc(wo_split, 1)
                for i, n in enumerate(("r", "k", "v")):
                    for kc in range(KC):
                        u = KC * i + kc
                        dve.wait_ge(w_hi_done, u + 1)
                        dve.tensor_tensor(lo[n][:, kc, :], bank[u % 8][:, :], f32(hi[n][:, kc, :]),
                                          ALU.subtract).then_inc(w_lo_done, 1)

                def residual_scales(g):
                    dve.tensor_scalar(xs[:, :, 0], ln1_stats[:, bass.ds(g * NT, NT), 1], RSQRT2, None,
                                      ALU.mult).then_inc(xs_step, 1)
                    dve.tensor_copy(st1[:, :, 0], ln1_stats[:, bass.ds(g * NT, NT), 0]).then_inc(xs_step, 1)
                    dve.wait_ge(xs_step, 3 * g + 2)
                    dve.scalar_tensor_tensor(xs[:, :, 1], st1[:, :, 0], -1.0, xs[:, :, 0], ALU.mult,
                                             ALU.mult).then_inc(xs_step, 1)
                    dve.wait_ge(xs_step, 3 * g + 3)
                    dve.tensor_scalar(xs[:, :, 0], xs[:, :, 0], 1.0, None, ALU.add).then_inc(xs_done, 1)

                def split_o(g):
                    dve.wait_ge(o_hi_done, g + 1)
                    dve.tensor_tensor(o_lo[:, :, :], o_raw[:, :, :], f32(o_hi[:, :, :]), ALU.subtract).then_inc(o_lo_done, 1)

                def store_y(g, t):
                    dve.wait_ge(y_done, 4 * g + t + 1)
                    dve.tensor_tensor(y[:, t, :], ps_y[t % 2][:, :], bo[:, :], ALU.add).then_inc(y_stored, 1)
                    dve.wait_ge(y_stored, 4 * g + t + 1)
                    dve.bn_stats(bn6[:, t, :], y[:, t, :]).then_inc(bn_step, 1)

                def aggregate(mv, done):
                    for t in range(NT):
                        ins = dve.bn_aggr(mv[:, t, :], bn6[:, t, :])
                    ins.then_inc(done, 1)

                def residual(g, par, t):
                    dve.scalar_tensor_tensor(y[:, t, :], y[:, t, :], mv_y[:, t, 0:1], gam[:, :], ALU.subtract,
                                             ALU.mult).then_inc(t1_done, 1)
                    dve.wait_ge(res_done, 4 * g + t + 1)
                    dve.wait_ge(t1_done, 4 * g + t + 1)
                    dve.scalar_tensor_tensor(x2[par][:, t, :], y[:, t, :], rstd_y[:, t:t + 1], xc[:, t, :], ALU.mult,
                                             ALU.add).then_inc(x2_done, 1)
                    dve.wait_ge(x2_done, 4 * g + t + 1)
                    dve.bn_stats(bn6[:, t, :], x2[par][:, t, :]).then_inc(bn2_step, 1)

                def activation_lo(f, d):
                    dve.wait_ge(act_hi_done, 4 * f + d + 1)
                    dve.tensor_tensor(relu[:, d % 2, :], relu[:, d % 2, :], relu[:, d % 2, :], ALU.mult).then_inc(sq_done, 1)
                    dve.wait_ge(sq_done, 4 * f + d + 1)
                    dve.tensor_tensor(act_lo[:, d, :], relu[:, d % 2, :], f32(act_hi[:, d, :]),
                                      ALU.subtract).then_inc(act_lo_done, 1)

                def gated(f, t):
                    dve.wait_ge(kv_done, 4 * f + t + 1)
                    dve.wait_ge(gate_done, 4 * f + t + 1)
                    dve.tensor_tensor(gate[:, t, :], ps_v[t % 2][:, :], gate[:, t, :], ALU.mult).then_inc(rkv_done, 1)

                def mix(g, n):
                    for kc in range(KC):
                        dve.wait_ge(before_done[n], 4 * g + kc + 1)
                        dve.scalar_tensor_tensor(mixed[:, kc, :], lnT[:, kc, 1:CHUNK + 1], mu[n][:, kc:kc + 1],
                                                 mixed[:, kc, :], ALU.mult, ALU.add).then_inc(mixed_done[n], 1)

                def mix_lo(g, n):
                    for kc in range(KC):
                        dve.wait_ge(m_hi_done[n], 4 * g + kc + 1)
                        dve.tensor_tensor(m_lo[n][:, kc, :], mixed[:, kc, :], f32(m_hi[n][:, kc, :]),
                                          ALU.subtract).then_inc(m_lo_done[n], 1)

                residual_scales(0)
                split_o(0)

                def step(g, par, first, second):
                    f = g - 1
                    if first:
                        for t in range(NT):
                            store_y(g, t)
                        dve.wait_ge(bn_step, 4 * g + 4)
                    if second:
                        activation_lo(f, 0)
                    if first:
                        aggregate(mv_y, bn_y)
                    if second:
                        activation_lo(f, 1)
                    if first:
                        dve.wait_ge(rstd_y_done, g + 1)
                    for t in range(NT):
                        if first:
                            residual(g, par, t)
                        if first and t == 3:
                            dve.wait_ge(bn2_step, 4 * g + 4)
                        if second and t >= 2:
                            activation_lo(f, t)
                        if first and t == 3:
                            aggregate(mv_2, bn_2)
                    more = first and not (isinstance(g, int) and g == CHUNKS - 1)
                    if more:
                        residual_scales(g + 1)
                    if first:
                        if par == 1:
                            dve.tensor_copy(lnT[:, :, 0:1], lnT[:, :, CHUNK:CHUNK + 1]).then_inc(prev_done, 1)
                        else:
                            dve.memset(lnT[:, :, 0:1], 0.0).then_inc(prev_done, 1)
                        dve.wait_ge(rstd_2_done, g + 1)
                        for t in range(NT):
                            dve.tensor_scalar(y[:, t, :], x2[par][:, t, :], mv_2[:, t, 0:1], rstd_2[:, t:t + 1],
                                              ALU.subtract, ALU.mult).then_inc(ln2_done, 1)
                    if more:
                        split_o(g + 1)
                    if first:
                        mix(g, "k")
                    if second:
                        gated(f, 0)
                    if first:
                        mix_lo(g, "k")
                    if second:
                        gated(f, 1)
                    if first:
                        mix(g, "r")
                    if second:
                        gated(f, 2)
                    if first:
                        mix_lo(g, "r")
                    if second:
                        gated(f, 3)

                over_steps(dve, step)

            @block.scalar
            def _(act):
                for i, n in enumerate(("r", "k", "v")):
                    for kc in range(KC):
                        u = KC * i + kc
                        act.wait_ge(w_turned, u + 1)
                        act.activation(hi[n][:, kc, :], bank[u % 8][:, :], ACT.Copy).then_inc(w_hi_done, 1)

                def split_o(g):
                    act.wait_ge(o_in, 16 * g + 16)
                    act.activation(o_hi[:, :, :], o_raw[:, :, :], ACT.Copy).then_inc(o_hi_done, 1)

                def mix_before(g, n, kc):
                    act.activation(mixed[:, kc, :], lnT[:, kc, 0:CHUNK], ACT.Copy,
                                   scale=mu1[n][:, kc:kc + 1]).then_inc(before_done[n], 1)

                def mix_hi(g, n, kc):
                    act.wait_ge(mixed_done[n], 4 * g + kc + 1)
                    act.activation(m_hi[n][:, kc, :], mixed[:, kc, :], ACT.Copy).then_inc(m_hi_done[n], 1)

                act.wait_ge(wo_split, 2)
                split_o(0)

                def step(g, par, first, second):
                    f = g - 1
                    if first:
                        act.wait_ge(x_in, 16 * g + 16)
                        act.wait_ge(xs_done, g + 1)
                        for t in range(NT):
                            act.activation(xc[:, t, :], xc[:, t, :], ACT.Identity, scale=xs[:, t, 0:1],
                                           bias=xs[:, t, 1:2]).then_inc(res_act, 1)
                    if second:
                        for d in range(KC):
                            act.wait_ge(k_done, 4 * f + d + 1)
                            if d >= 2:
                                act.wait_ge(act_lo_done, 4 * f + d - 1)
                            act.activation(relu[:, d % 2, :], ps_k[d % 2][:, :], ACT.Relu).then_inc(relu_done, 1)
                            act.wait_ge(relu_done, 4 * f + d + 1)
                            act.activation(act_hi[:, d, :], relu[:, d % 2, :], ACT.Square).then_inc(act_hi_done, 1)
                    if first and not (isinstance(g, int) and g == CHUNKS - 1):
                        act.wait_ge(y_done, 4 * g + 4)
                        split_o(g + 1)
                    if second:
                        for t in range(NT):
                            act.wait_ge(r_done, 4 * f + t + 1)
                            if not (isinstance(g, int) and g == 1):
                                act.wait_ge(out_done, 64 * f)
                            act.activation(gate[:, t, :], ps_r[t % 2][:, :], ACT.Sigmoid).then_inc(gate_done, 1)
                    if first:
                        for t in range(NT):
                            act.wait_ge(ln2_turned, 4 * g + t + 1)
                            if t == 0:
                                act.wait_ge(prev_done, g + 1)
                            act.activation(lnT[:, :, 1 + t * P:1 + (t + 1) * P],
                                           ps_y[t % 2][:, :].rearrange("p (k n) -> p k n", k=KC),
                                           ACT.Copy).then_inc(lnT_done, 1)
                        act.wait_ge(lnT_done, 4 * g + 4)
                        for kc in range(KC):
                            mix_before(g, "k", kc)
                        for kc in range(KC):
                            mix_hi(g, "k", kc)
                        for kc in range(KC):
                            act.wait_ge(m_lo_done["k"], 4 * g + kc + 1)
                            mix_before(g, "r", kc)
                        for kc in range(KC):
                            mix_hi(g, "r", kc)

                over_steps(act, step)

            @block.tensor
            def _(pe):
                for i, n in enumerate(("r", "k", "v")):
                    pe.wait_ge(w_in[i + 1], 16)
                    for kc in range(KC):
                        u = KC * i + kc
                        if u >= 8:
                            pe.wait_ge(w_lo_done, u - 7)
                        for d in range(KC):
                            ins = pe.transpose(bank[u % 8][:, d * P:(d + 1) * P], raw[n][:, d, kc * P:(kc + 1) * P],
                                               ident[:, :])
                        ins.then_inc(w_turned, 1)
                pe.wait_ge(w_lo_done, 3 * KC)

                def product(out, a_hi, a_lo, b_hi, b_lo, a_cols, b_cols, done):
                    prods = [(a, b, kc) for kc in range(KC) for a, b in ((a_lo, b_hi), (a_hi, b_lo), (a_hi, b_hi))]
                    for i, (a, b, kc) in enumerate(prods):
                        ins = pe.matmul(out, a[:, kc, a_cols], b[:, kc, b_cols], start=(i == 0), stop=(i == len(prods) - 1))
                    ins.then_inc(done, 1)

                whole = slice(0, C)

                def step(g, par, first, second):
                    f = g - 1
                    if first:
                        pe.wait_ge(o_hi_done, g + 1)
                        pe.wait_ge(o_lo_done, g + 1)
                        for t in range(NT):
                            if t < 2 and second:
                                pe.wait_ge(lnT_done, 4 * g - 1 + t)
                            if t >= 2:
                                pe.wait_ge(y_stored, 4 * g + t - 1)
                            product(ps_y[t % 2][:, :], o_hi, o_lo, hi["out"], lo["out"], slice(t * P, (t + 1) * P), whole, y_done)
                    if second:
                        pe.wait_ge(m_hi_done["k"], 4 * f + 4)
                        pe.wait_ge(m_lo_done["k"], 4 * f + 4)
                        for d in range(KC):
                            if d >= 2:
                                pe.wait_ge(relu_done, 4 * f + d - 1)
                            product(ps_k[d % 2][:, :], hi["k"], lo["k"], m_hi["k"], m_lo["k"], slice(d * P, (d + 1) * P), whole, k_done)
                        pe.wait_ge(m_hi_done["r"], 4 * f + 4)
                        pe.wait_ge(m_lo_done["r"], 4 * f + 4)
                        for t in range(NT):
                            if t >= 2:
                                pe.wait_ge(gate_done, 4 * f + t - 1)
                            product(ps_r[t % 2][:, :], m_hi["r"], m_lo["r"], hi["r"], lo["r"], slice(t * P, (t + 1) * P), whole, r_done)
                    if first:
                        for t in range(NT):
                            pe.wait_ge(ln2_done, 4 * g + t + 1)
                            if t < 2:
                                pe.wait_ge(y_stored, 4 * g + t + 3)
                            else:
                                pe.wait_ge(lnT_done, 4 * g + t - 1)
                            for k in range(KC):
                                ins = pe.transpose(ps_y[t % 2][:, k * P:(k + 1) * P], y[:, t, k * P:(k + 1) * P], ident[:, :])
                            ins.then_inc(ln2_turned, 1)
                    if second:
                        pe.wait_ge(act_lo_done, 4 * f + 4)
                        for t in range(NT):
                            if t >= 2:
                                pe.wait_ge(rkv_done, 4 * f + t - 1)
                            product(ps_v[t % 2][:, :], act_hi, act_lo, hi["v"], lo["v"], slice(t * P, (t + 1) * P), whole, kv_done)

                over_steps(pe, step)


def seq_preln_block(nc, x, w_qk, b_qk, w_v, b_v, w_out, b_out, gamma, beta, w_r, w_k, w_v2, mu_r, mu_k, out):
    with ExitStack() as ctx:
        ident = ctx.enter_context(nc.sbuf_tensor("ident", [P, P], F32))
        ln1_stats = ctx.enter_context(nc.sbuf_tensor("ln1_stats", [P, B * TT, 2], F32))
        o_scratch = nc.dram_tensor("o_scratch", [B, 2, HEADS, DH, HALF], F32, kind="Internal").ap()
        attention_pass(nc, x, w_qk, b_qk, w_v, b_v, o_scratch, ln1_stats, ident)
        mix_pass(nc, x, o_scratch, w_out, b_out, gamma, beta, w_r, w_k, w_v2, mu_r, mu_k, out, ln1_stats, ident)


_INS = ["L0_attn_x", "L0_attn_W_qk", "L0_attn_b_qk", "L0_attn_W_v", "L0_attn_b_v", "L0_attn_W_out", "L0_attn_b_out",
        "L0_attn_ln_gamma", "L0_attn_ln_beta", "L0_ffn_W_r", "L0_ffn_W_k", "L0_ffn_W_v", "L0_ffn_mu_r", "L0_ffn_mu_k"]


def kernel(**inputs):
    import numpy as _np
    import concourse.bacc as _bacc
    from concourse import mybir as _mybir
    from concourse.bass_utils import run_bass_kernel_spmd as _run

    nc = _bacc.Bacc("TRN2", target_bir_lowering=False, num_devices=1)
    arrays, args = {}, []
    for name in _INS:
        a = _np.ascontiguousarray(inputs[name])
        arrays[f"in_{name}_dram"] = a
        args.append(nc.dram_tensor(f"in_{name}_dram", a.shape, _mybir.dt.from_np(a.dtype), kind="ExternalInput").ap())
    args.append(nc.dram_tensor("out_dram", [B, T, C], F32, kind="ExternalOutput").ap())
    seq_preln_block(nc, *args)
    r = _run(nc, [arrays], core_ids=[0])
    return r.results[0]["out_dram"]
```

```python
from contextlib import ExitStack

import concourse.bass as bass
from concourse import mybir

F32 = mybir.dt.float32
F32R = mybir.dt.float32r
ALU = mybir.AluOpType
ACT = mybir.ActivationFunctionType
AX_X = mybir.AxisListType.X

P = 128
B, T, C = 8, 1024, 512
HEADS, DH = 8, 64
KC = C // P
TT = T // P
HALF = T // 2
SLOTS = HEADS * TT
LAST_SLOT = SLOTS + 6
XHAT_TURNS = [55, 56, 57, 58, 62, 63, 64, 65]
V_SLOTS = [0, 0, 1, 1, 2, 3, 4, 5]
QK_STORES = [2, 5]
NEXT_QK_STORES = [61, 66]
STATS_SLOT = 38
QUAD = 4
EPS = 1e-5
RSQRT2 = 2.0 ** -0.5
SCALE = DH ** -0.5


def f32(ap):
    return ap.bitcast(F32)


def chunks_of(o_scratch):
    return o_scratch.rearrange("b c h d t -> (b c) (h d) t").rearrange("g (k p) t -> g p k t", p=P)


def query_tile(r):
    return r // 2 + (TT // 2) * (r % 2)


def attention_pass(nc, x, w_qk, b_qk, w_v, b_v, w_out, w_r, w_out_raw, stage, o_scratch, ln1_stats, ident):
    with ExitStack() as ctx:
        def sb(name, shape, dt=F32):
            return ctx.enter_context(nc.sbuf_tensor(name, shape, dt))

        def sem(name):
            return ctx.enter_context(nc.semaphore(name))

        wqk_hi = sb("wqk_hi", [P, KC, HEADS, 2, DH], F32R)
        wqk_lo = sb("wqk_lo", [P, KC, HEADS, 2, DH], F32R)
        wv_hi = sb("wv_hi", [P, KC, C], F32R)
        wv_lo = sb("wv_lo", [P, KC, C], F32R)
        bqk = sb("bqk", [P, HEADS])
        bv = sb("bv", [P, C])
        xT_hi = sb("xT_hi", [P, KC, T], F32R)
        xT_lo = sb("xT_lo", [P, KC, T], F32R)
        q_hilo = [sb(f"q_hilo{i}", [P, T], F32R) for i in range(2)]
        k_hihi = [sb(f"k_hihi{i}", [P, T], F32R) for i in range(2)]
        k_lolo = [sb(f"k_lolo{i}", [P, T], F32R) for i in range(2)]
        v = sb("v", [P, TT, C])
        probs = [sb(f"probs{i}", [P, T]) for i in range(3)]
        probsT = sb("probsT", [P, 2, TT, 2, 2 * P])
        neg_max = sb("neg_max", [P, 2, TT])
        row_sum = sb("row_sum", [P, 2, TT])
        row_inv = sb("row_inv", [P, 2, TT])
        inv_wide = sb("inv_wide", [P, 2, TT, DH])
        inv_cols = sb("inv_cols", [P, HALF])
        oT = [sb(f"oT{i}", [P, HALF]) for i in range(2)]
        xb = stage[:, :, :, :].rearrange("p a k n -> p (a k) n")
        xhat = [sb(f"xhat{i}", [P, C]) for i in range(2)]
        bn6 = sb("bn6", [P, TT, 6])
        mean_var = sb("mean_var", [P, TT, 2])
        rstd = sb("rstd", [P, TT])
        neg_half = sb("neg_half", [P, TT])
        eps = sb("eps", [P, TT])
        wqk_raw = probsT[:, 0].rearrange("p a b c -> p (a b c)").rearrange("p (k h d s) -> p k h d s", k=KC, h=HEADS, s=2)
        wv_raw = probsT[:, 1].rearrange("p a b c -> p (a b c)")[:, 0:KC * C].rearrange("p (k n) -> p k n", k=KC)

        ps_scores = [ctx.enter_context(nc.psum_tensor(f"ps_scores{i}", [P, T], F32)) for i in range(2)]
        ps_turnA = ctx.enter_context(nc.psum_tensor("ps_turnA", [P, 4, P], F32))
        ps_turnB = ctx.enter_context(nc.psum_tensor("ps_turnB", [P, 4, P], F32))
        ps_o = ctx.enter_context(nc.psum_tensor("ps_o", [P, HALF], F32))
        ps_misc = ctx.enter_context(nc.psum_tensor("ps_misc", [P, HALF], F32))
        turnA_bank = ps_turnA[:, :, :].rearrange("p a b -> p (a b)")
        turnB_bank = ps_turnB[:, :, :].rearrange("p a b -> p (a b)")
        v_banks = [turnA_bank, turnB_bank, turnA_bank] + [ps_o[:, :]] * 5
        misc4 = ps_misc[:, :].rearrange("p (k n) -> p k n", k=KC)
        first_turns = [misc4, ps_turnA[:, :, :], ps_turnB[:, :, :], ps_o[:, :].rearrange("p (k n) -> p k n", k=KC)]

        wqk_in = [sem(f"wqk_in{i}") for i in range(KC)]
        wv_in = sem("wv_in")
        b_in = sem("b_in")
        pass2_in = sem("pass2_in")
        bqk_done = sem("bqk_done")
        wq_scaled = sem("wq_scaled")
        wq_hi_done = sem("wq_hi_done")
        wq_lo_done = sem("wq_lo_done")
        wk_hi_done = sem("wk_hi_done")
        wk_lo_done = sem("wk_lo_done")
        wv_hi_done = sem("wv_hi_done")
        wv_lo_done = sem("wv_lo_done")
        x_in = [sem(f"x_in{i}") for i in range(4)]
        bn_done = sem("bn_done")
        bn_step = sem("bn_step")
        eps_done = sem("eps_done")
        rstd_done = sem("rstd_done")
        half_set = sem("half_set")
        xhat_done = sem("xhat_done")
        xhatT_done = sem("xhatT_done")
        xT_hi_done = sem("xT_hi_done")
        xT_lo_done = sem("xT_lo_done")
        qk_done = sem("qk_done")
        qk_hi_done = sem("qk_hi_done")
        k_lo_done = sem("k_lo_done")
        qk_lo_done = sem("qk_lo_done")
        k_copied = [sem(f"k_copied{i}") for i in range(2)]
        v_done = sem("v_done")
        v_stored = sem("v_stored")
        scores_done = sem("scores_done")
        max_done = sem("max_done")
        exp_done = sem("exp_done")
        turnA_done = sem("turnA_done")
        turnB_done = sem("turnB_done")
        turnA_stored = sem("turnA_stored")
        turnB_stored = sem("turnB_stored")
        pv_done = sem("pv_done")
        recip_done = sem("recip_done")
        inv_done = sem("inv_done")
        inv_turned = sem("inv_turned")
        inv_stored = sem("inv_stored")
        o_done = sem("o_done")
        oT_free = [sem(f"oT_free{i}") for i in range(2)]
        ident_set = sem("ident_set")
        stats_kept = sem("stats_kept")

        x_tiles = x.rearrange("b (t p) c -> b p t c", p=P)

        with nc.Block() as block:

            @block.sync
            def _(sp):
                def load_x(b, i):
                    sp.dma_start(xb[:, 2 * i:2 * i + 2, :], x_tiles[b][:, 2 * i:2 * i + 2, :]).then_inc(x_in[i], 16)

                for i in range(4):
                    load_x(0, i)
                wqk_view = w_qk.rearrange("(k p) (h d s) -> k p h d s", p=P, h=HEADS, s=2)
                for kc in range(KC):
                    sp.dma_start(wqk_raw[:, kc], wqk_view[kc]).then_inc(wqk_in[kc], 16)
                bqk_view = b_qk.rearrange("(h d s) -> s d h", h=HEADS, s=2)
                for s in range(2):
                    sp.dma_start(bqk[s * DH:(s + 1) * DH, :], bqk_view[s], allow_slow_non_contiguous=True).then_inc(b_in, 16)
                sp.dma_start(wv_raw, w_v.rearrange("(k p) n -> p k n", p=P)).then_inc(wv_in, 16)
                sp.dma_start(bv[:, :], b_v.rearrange("(o n) -> o n", o=1).broadcast_to([P, C])).then_inc(b_in, 16)

                def copy_k(b, h):
                    sp.wait_ge(k_lo_done, 16 * b + 2 * h + 2)
                    sp.dma_start(f32(k_hihi[h % 2][0:DH, :]), f32(k_hihi[h % 2][DH:P, :])).then_inc(k_copied[h % 2], 16)
                    sp.dma_start(f32(k_lolo[h % 2][0:DH, :]), f32(k_lolo[h % 2][DH:P, :])).then_inc(k_copied[h % 2], 16)

                def store_o(b, h):
                    sp.wait_ge(o_done, 8 * b + h + 1)
                    for half in range(2):
                        sp.dma_start(o_scratch[b][half, h, :, :],
                                     oT[h % 2][half * DH:(half + 1) * DH, :]).then_inc(oT_free[h % 2], 16)

                copy_k(0, 0)
                sp.dma_start(w_out_raw[:, :, :], w_out.rearrange("(k p) n -> p k n", p=P)).then_inc(pass2_in, 16)

                def entry(b, last):
                    for h in range(HEADS + 1):
                        if h == 0 and not last:
                            sp.wait_ge(xhat_done, 8 * b + 8)
                        if h < 4 and not last:
                            load_x(b + 1, h)
                        if h < HEADS - 1:
                            copy_k(b, h + 1)
                        if h == HEADS and not last:
                            copy_k(b + 1, 0)
                        if h == 4 and last:
                            sp.wait_ge(xhat_done, 8 * B)
                            for i in range(2):
                                sp.wait_ge(oT_free[i], 16 + 128)
                            sp.dma_start(stage[:, 0], chunks_of(o_scratch)[0]).then_inc(pass2_in, 16)
                            sp.dma_start(stage[:, 1], w_r.rearrange("(k p) n -> p k n", p=P)).then_inc(pass2_in, 16)
                        if h >= 1:
                            store_o(b, h - 1)

                with sp.Fori(0, B - 1) as b:
                    entry(b, False)
                entry(B - 1, True)
                sp.wait_ge(pass2_in, 48)
                for i in range(2):
                    sp.wait_ge(oT_free[i], 16 + 128 * B)

            @block.gpsimd
            def _(pool):
                pool.memset(ident[:, :], 0.0).then_inc(ident_set, 1)
                pool.wait_ge(ident_set, 1)
                pool.affine_select(out=ident[:, :], in_=ident[:, :], compare_op=ALU.not_equal, fill=1.0, base=0,
                                   pattern=[[-1, P]], channel_multiplier=1).then_inc(ident_set, 1)
                pool.memset(neg_half[:, :], -0.5).then_inc(half_set, 1)
                pool.memset(eps[:, :], EPS).then_inc(half_set, 1)
                pool.wait_ge(half_set, 2)

                def rstd_of(b):
                    pool.wait_ge(bn_done, b + 1)
                    pool.tensor_tensor(rstd[:, :], mean_var[:, :, 1], eps[:, :], ALU.add).then_inc(eps_done, 1)
                    pool.wait_ge(eps_done, b + 1)
                    pool.tensor_tensor(rstd[:, :], rstd[:, :], neg_half[:, :], ALU.pow).then_inc(rstd_done, 1)

                rstd_of(0)
                for kc in range(KC):
                    pool.wait_ge(wk_hi_done, kc + 1)
                    pool.tensor_tensor(wqk_lo[:, kc, :, 1, :], wqk_raw[:, kc, :, :, 1], f32(wqk_hi[:, kc, :, 1, :]),
                                       ALU.subtract).then_inc(wk_lo_done, 1)
                for kc in range(KC):
                    pool.wait_ge(wq_hi_done, kc + 1)
                    pool.tensor_tensor(wqk_lo[:, kc, :, 0, :], wqk_raw[:, kc, :, :, 0], f32(wqk_hi[:, kc, :, 0, :]),
                                       ALU.subtract).then_inc(wq_lo_done, 1)
                pool.wait_ge(wv_hi_done, 1)
                pool.tensor_tensor(wv_lo[:, :, :], wv_raw, f32(wv_hi[:, :, :]), ALU.subtract).then_inc(wv_lo_done, 1)
                with pool.Fori(0, B - 1) as b:
                    rstd_of(b + 1)

            @block.vector
            def _(dve):
                for i in range(2):
                    dve.memset(oT[i][:, :], 0.0).then_inc(oT_free[i], 16)
                def stats(b, t):
                    dve.wait_ge(x_in[t // 2], 16 * b + 16)
                    dve.bn_stats(bn6[:, t, :], xb[:, t, :]).then_inc(bn_step, 1)

                def aggregate():
                    for t in range(TT):
                        ins = dve.bn_aggr(mean_var[:, t, :], bn6[:, t, :])
                    ins.then_inc(bn_done, 1)

                def keep_stats(b):
                    dve.wait_ge(rstd_done, b + 1)
                    dve.tensor_copy(ln1_stats[:, bass.ds(b * TT, TT), 0], mean_var[:, :, 0])
                    dve.tensor_copy(ln1_stats[:, bass.ds(b * TT, TT), 1], rstd[:, :]).then_inc(stats_kept, 1)

                def normalise(b, t):
                    if t >= 2:
                        dve.wait_ge(xhatT_done, 8 * b + t - 1)
                    dve.tensor_scalar(xhat[t % 2][:, :], xb[:, t, :], mean_var[:, t, 0:1], rstd[:, t:t + 1],
                                      ALU.subtract, ALU.mult).then_inc(xhat_done, 1)

                def store_xT_lo(b, t, turned):
                    dve.wait_ge(xT_hi_done, 8 * b + t + 1)
                    cols = slice(t * P, (t + 1) * P)
                    dve.tensor_tensor(xT_lo[:, :, cols], turned, f32(xT_hi[:, :, cols]),
                                      ALU.subtract).then_inc(xT_lo_done, 1)

                def store_k_lo(b, h, half, ps=ps_misc):
                    dve.wait_ge(qk_hi_done, 16 * b + 2 * h + half + 1)
                    cols = slice(half * HALF, (half + 1) * HALF)
                    i = h % 2
                    dve.scalar_tensor_tensor(k_lolo[i][DH:P, cols], ps[DH:P, :], bqk[DH:P, h:h + 1],
                                             f32(k_hihi[i][DH:P, cols]), ALU.add, ALU.subtract).then_inc(k_lo_done, 1)

                def store_q_lo(b, h, half, ps=ps_misc):
                    cols = slice(half * HALF, (half + 1) * HALF)
                    i = h % 2
                    dve.scalar_tensor_tensor(q_hilo[i][DH:P, cols], ps[0:DH, :], bqk[0:DH, h:h + 1],
                                             f32(q_hilo[i][0:DH, cols]), ALU.add, ALU.subtract).then_inc(qk_lo_done, 1)

                def store_v(b, t):
                    dve.wait_ge(v_done, 8 * b + t + 1)
                    dve.tensor_tensor(v[:, t, :], v_banks[t], bv[:, :], ALU.add).then_inc(v_stored, 1)

                for t in range(TT):
                    stats(0, t)
                dve.wait_ge(bn_step, TT)
                aggregate()
                keep_stats(0)
                for t in range(TT):
                    normalise(0, t)
                    if t >= 2:
                        store_xT_lo(0, t - 2, first_turns[(t - 2) % 4])
                dve.wait_ge(b_in, 48)
                dve.tensor_scalar(bqk[0:DH, :], bqk[0:DH, :], SCALE, None, ALU.mult).then_inc(bqk_done, 1)
                for t in (TT - 2, TT - 1):
                    store_xT_lo(0, t, first_turns[t % 4])
                for half in range(2):
                    store_k_lo(0, 0, half, (ps_misc, ps_o)[half])
                    store_q_lo(0, 0, half, (ps_misc, ps_o)[half])

                def entry(b, last):
                    for n in range(LAST_SLOT):
                        h, r = n // TT, n % TT
                        if n == STATS_SLOT + TT and not last:
                            dve.wait_ge(bn_step, 8 * b + 16)
                        if n == 0:
                            store_v(b, 0)
                            store_v(b, 1)
                        if n < SLOTS:
                            dve.wait_ge(scores_done, 64 * b + n + 1)
                            dve.tensor_reduce(neg_max[:, h % 2, r:r + 1], ps_scores[n % 2][:, :], AX_X, ALU.max,
                                              negate=True).then_inc(max_done, 1)
                        for t in range(TT):
                            if V_SLOTS[t] == n and n > 0:
                                store_v(b, t)
                        if r == 1 and h >= 1:
                            dve.wait_ge(exp_done, 64 * b + 8 * h)
                            dve.reciprocal(row_inv[:, (h - 1) % 2, :], row_sum[:, (h - 1) % 2, :]).then_inc(recip_done, 1)
                            dve.wait_ge(recip_done, 8 * b + h)
                            dve.tensor_copy(inv_wide[:, (h - 1) % 2, :, :],
                                            row_inv[:, (h - 1) % 2, :].unsqueeze(2).broadcast_to([P, TT, DH])).then_inc(inv_done, 1)
                        if h < HEADS - 1:
                            if r in QK_STORES:
                                store_k_lo(b, h + 1, QK_STORES.index(r))
                            if r == QK_STORES[0]:
                                store_q_lo(b, h + 1, 0)
                            if r == QK_STORES[1] + 1:
                                store_q_lo(b, h + 1, 1)
                        if n in NEXT_QK_STORES and not last:
                            store_k_lo(b + 1, 0, NEXT_QK_STORES.index(n))
                            store_q_lo(b + 1, 0, NEXT_QK_STORES.index(n))
                        if not last and n in XHAT_TURNS:
                            store_xT_lo(b + 1, XHAT_TURNS.index(n), misc4)
                        if 2 <= n < SLOTS + 2:
                            m = n - 2
                            dve.wait_ge(turnB_done, 64 * b + m + 1)
                            dve.tensor_copy(probsT[:, m // QUAD % 2, 4:8, m % 2, m % QUAD // 2 * P:(m % QUAD // 2 + 1) * P],
                                            ps_turnB[:, :, :]).then_inc(turnB_stored, 1)
                        if not last:
                            if STATS_SLOT <= n < STATS_SLOT + TT:
                                stats(b + 1, n - STATS_SLOT)
                            if n == STATS_SLOT + TT:
                                aggregate()
                            if n == XHAT_TURNS[0] - 4:
                                keep_stats(b + 1)
                            if XHAT_TURNS[0] - 3 <= n < XHAT_TURNS[0] - 1:
                                normalise(b + 1, n - XHAT_TURNS[0] + 3)
                            if n in XHAT_TURNS[:-2]:
                                normalise(b + 1, XHAT_TURNS.index(n) + 2)
                        if r == 5 and h >= 1:
                            dve.wait_ge(pv_done, 8 * b + h)
                            dve.wait_ge(inv_stored, 8 * b + h)
                            dve.wait_ge(oT_free[(h - 1) % 2], 128 * b + 16 + 32 * ((h - 1) // 2))
                            dve.tensor_tensor(oT[(h - 1) % 2][:, :], ps_o[:, :], inv_cols[:, :],
                                              ALU.mult).then_inc(o_done, 1)

                with dve.Fori(0, B - 1) as b:
                    entry(b, False)
                entry(B - 1, True)

            @block.scalar
            def _(act):
                def split_wqk(kc):
                    act.wait_ge(wqk_in[kc], 16)
                    act.activation(wqk_hi[:, kc, :, 1, :], wqk_raw[:, kc, :, :, 1], ACT.Copy).then_inc(wk_hi_done, 1)
                    act.activation(wqk_raw[:, kc, :, :, 0], wqk_raw[:, kc, :, :, 0], ACT.Copy,
                                   scale=SCALE).then_inc(wq_scaled, 1)
                    act.wait_ge(wq_scaled, kc + 1)
                    act.activation(wqk_hi[:, kc, :, 0, :], wqk_raw[:, kc, :, :, 0], ACT.Copy).then_inc(wq_hi_done, 1)

                def store_xT_hi(b, t, turned):
                    act.wait_ge(xhatT_done, 8 * b + t + 1)
                    act.activation(xT_hi[:, :, t * P:(t + 1) * P], turned, ACT.Copy).then_inc(xT_hi_done, 1)

                def store_qk_hi(b, h, half, ps=ps_misc):
                    act.wait_ge(qk_done, 16 * b + 2 * h + half + 1)
                    cols = slice(half * HALF, (half + 1) * HALF)
                    i = h % 2
                    act.activation(q_hilo[i][0:DH, cols], ps[0:DH, :], ACT.Identity, bias=bqk[0:DH, h:h + 1])
                    act.activation(k_hihi[i][DH:P, cols], ps[DH:P, :], ACT.Identity,
                                   bias=bqk[DH:P, h:h + 1]).then_inc(qk_hi_done, 1)

                def store_inv(b, h, turned=ps_misc[:, :]):
                    act.wait_ge(inv_turned, 8 * b + h)
                    if h >= 2:
                        act.wait_ge(o_done, 8 * b + h - 1)
                    act.activation(inv_cols[:, :], turned, ACT.Copy).then_inc(inv_stored, 1)

                for kc in range(KC - 1):
                    split_wqk(kc)
                for t in range(TT):
                    store_xT_hi(0, t, first_turns[t % 4])
                    if t == 1:
                        split_wqk(KC - 1)
                act.wait_ge(wv_in, 16)
                act.activation(wv_hi[:, :, :], wv_raw, ACT.Copy).then_inc(wv_hi_done, 1)
                act.wait_ge(bqk_done, 1)
                for half in range(2):
                    store_qk_hi(0, 0, half, (ps_misc, ps_o)[half])

                def entry(b, last):
                    for n in range(LAST_SLOT):
                        h, r = n // TT, n % TT
                        if 1 <= n <= SLOTS:
                            m = n - 1
                            act.wait_ge(max_done, 64 * b + m + 1)
                            if m >= 3:
                                act.wait_ge(turnB_done, 64 * b + m - 2)
                            act.activation(probs[m % 3][:, :], ps_scores[m % 2][:, :], ACT.Exp,
                                           bias=neg_max[:, m // TT % 2, m % TT:m % TT + 1],
                                           accum_out=row_sum[:, m // TT % 2, m % TT:m % TT + 1]).then_inc(exp_done, 1)
                        if r in QK_STORES and h < HEADS - 1:
                            store_qk_hi(b, h + 1, QK_STORES.index(r))
                        if n in NEXT_QK_STORES and not last:
                            store_qk_hi(b + 1, 0, NEXT_QK_STORES.index(n))
                        if not last and n in XHAT_TURNS:
                            store_xT_hi(b + 1, XHAT_TURNS.index(n), misc4)
                        if 2 <= n < SLOTS + 2:
                            m = n - 2
                            act.wait_ge(turnA_done, 64 * b + m + 1)
                            act.activation(probsT[:, m // QUAD % 2, 0:4, m % 2, m % QUAD // 2 * P:(m % QUAD // 2 + 1) * P],
                                           ps_turnA[:, :, :], ACT.Copy).then_inc(turnA_stored, 1)
                        if r == 3 and 1 <= h < HEADS:
                            store_inv(b, h)
                        if n == SLOTS + 2:
                            store_inv(b, HEADS, turnA_bank)

                with act.Fori(0, B - 1) as b:
                    entry(b, False)
                entry(B - 1, True)

            @block.tensor
            def _(pe):
                def turn_xhat(b, t, turned):
                    pe.wait_ge(xhat_done, 8 * b + t + 1)
                    for k in range(KC):
                        ins = pe.transpose(turned[:, k, :], xhat[t % 2][:, k * P:(k + 1) * P], ident[:, :])
                    ins.then_inc(xhatT_done, 1)

                def project_qk(b, h, half, first, end, ps=ps_misc):
                    cols = slice(half * HALF, (half + 1) * HALF)
                    prods = [(w, xt, kc) for kc in range(KC) for w, xt in ((wqk_lo, xT_hi), (wqk_hi, xT_lo), (wqk_hi, xT_hi))]
                    for n in range(first, end):
                        w, xt, kc = prods[n]
                        ins = pe.matmul(ps[:, :], w[:, kc, h, :, :].rearrange("p s d -> p (s d)"), xt[:, kc, cols],
                                        start=(n == 0), stop=(n == 11))
                    if end == 12:
                        ins.then_inc(qk_done, 1)

                def misc_free_of_qk(b, h, half):
                    pe.wait_ge(qk_hi_done, 16 * b + 2 * h + half + 1)
                    pe.wait_ge(qk_lo_done, 16 * b + 2 * h + half + 1)

                def misc_free_of_xhat(b, t):
                    pe.wait_ge(xT_hi_done, 8 * b + t + 1)
                    pe.wait_ge(xT_lo_done, 8 * b + t + 1)

                pe.wait_ge(ident_set, 2)
                for t in range(TT):
                    if t >= 4:
                        misc_free_of_xhat(0, t - 4)
                    turn_xhat(0, t, first_turns[t % 4])
                misc_free_of_xhat(0, TT - 1)
                pe.wait_ge(wk_lo_done, KC)
                pe.wait_ge(wq_lo_done, KC)
                for half in range(2):
                    project_qk(0, 0, half, 0, 12, (ps_misc, ps_o)[half])
                pe.wait_ge(wv_lo_done, 1)

                def project_v(b, t):
                    prods = [(xt, w, kc) for kc in range(KC) for xt, w in ((xT_lo, wv_hi), (xT_hi, wv_lo), (xT_hi, wv_hi))]
                    for i, (xt, w, kc) in enumerate(prods):
                        ins = pe.matmul(v_banks[t], xt[:, kc, t * P:(t + 1) * P], w[:, kc, :], start=(i == 0), stop=(i == 11))
                    ins.then_inc(v_done, 1)

                def scores(b, n):
                    h, r = n // TT, n % TT
                    if r == 0:
                        pe.wait_ge(qk_lo_done, 16 * b + 2 * h + 2)
                        pe.wait_ge(k_copied[h % 2], 128 * b + 32 * (h // 2) + 32)
                    if n >= 2:
                        pe.wait_ge(exp_done, 64 * b + n - 1)
                    tile = slice(query_tile(r) * P, (query_tile(r) + 1) * P)
                    for half in range(2):
                        cols = slice(half * HALF, (half + 1) * HALF)
                        for i, k in enumerate((k_lolo, k_hihi)):
                            ins = pe.matmul(ps_scores[n % 2][:, cols], q_hilo[h % 2][:, tile], k[h % 2][:, cols],
                                            start=(i == 0), stop=(i == 1))
                    ins.then_inc(scores_done, 1)

                def turn_probs(b, m):
                    pe.wait_ge(exp_done, 64 * b + m + 1)
                    for ps, first, stored, done in ((ps_turnA, 0, turnA_stored, turnA_done),
                                                    (ps_turnB, 4, turnB_stored, turnB_done)):
                        if m >= 1:
                            pe.wait_ge(stored, 64 * b + m)
                        for j in range(4):
                            ins = pe.transpose(ps[:, j, :], probs[m % 3][:, (first + j) * P:(first + j + 1) * P], ident[:, :])
                        ins.then_inc(done, 1)

                def p_at_v(b, quad, part):
                    h, q2 = quad // 2, quad % 2
                    if part == 0:
                        pe.wait_ge(turnA_stored, 64 * b + QUAD * quad + QUAD)
                        pe.wait_ge(turnB_stored, 64 * b + QUAD * quad + QUAD)
                        if q2 == 0 and h >= 1:
                            pe.wait_ge(o_done, 8 * b + h)
                    for jt in (2 * part, 2 * part + 1):
                        for half in range(2):
                            ins = pe.matmul(ps_o[half * DH:(half + 1) * DH, q2 * 2 * P:(q2 + 1) * 2 * P],
                                            v[:, jt, h * DH:(h + 1) * DH], probsT[:, quad % 2, jt, half, :],
                                            start=(jt == 0), stop=(jt == TT - 1))
                    if part == 3 and q2 == 1:
                        ins.then_inc(pv_done, 1)

                def spread_inv(b, h, turned=ps_misc[:, :]):
                    pe.wait_ge(inv_done, 8 * b + h + 1)
                    for m in range(4):
                        cols = inv_wide[:, h % 2, 2 * m:2 * m + 2, :].rearrange("p r d -> p (r d)")
                        ins = pe.transpose(turned[:, m * P:(m + 1) * P], cols, ident[:, :])
                    ins.then_inc(inv_turned, 1)

                def entry(b, last):
                    for n in range(LAST_SLOT):
                        h, r = n // TT, n % TT
                        if n == 0:
                            project_v(b, 0)
                            project_v(b, 1)
                        if n < SLOTS:
                            scores(b, n)
                        if not last and n in XHAT_TURNS:
                            t = XHAT_TURNS.index(n)
                            if t == 0:
                                misc_free_of_qk(b, HEADS - 1, 1)
                            elif t == 4:
                                misc_free_of_qk(b + 1, 0, 0)
                            else:
                                misc_free_of_xhat(b + 1, t - 1)
                            turn_xhat(b + 1, t, misc4)
                        for t in range(TT):
                            if V_SLOTS[t] == n and n > 0:
                                if t in (2, 4, 5, 6, 7):
                                    pe.wait_ge(v_stored, 8 * b + (1 if t == 2 else t))
                                project_v(b, t)
                        if r == 3 and 1 <= h < HEADS:
                            if h < HEADS - 1:
                                misc_free_of_qk(b, h + 1, 0)
                            elif last:
                                misc_free_of_qk(b, h, 1)
                            else:
                                misc_free_of_xhat(b + 1, 3)
                            spread_inv(b, h - 1)
                        if n == 2:
                            pe.wait_ge(v_stored, 8 * b + 3)
                        if 2 <= n < SLOTS + 2:
                            turn_probs(b, n - 2)
                        if n == 6:
                            pe.wait_ge(v_stored, 8 * b + TT)
                        if n >= 6:
                            p_at_v(b, (n - 6) // QUAD, (n - 6) % QUAD)
                        if h < HEADS - 1:
                            if n == 0:
                                misc_free_of_qk(b, 0, 1)
                                project_qk(b, 1, 0, 0, 4)
                            if r == 0:
                                project_qk(b, h + 1, 0, 4, 8)
                            if r == 1:
                                project_qk(b, h + 1, 0, 8, 12)
                            if r == 3:
                                misc_free_of_qk(b, h + 1, 0)
                                if h >= 1:
                                    pe.wait_ge(inv_stored, 8 * b + h)
                                project_qk(b, h + 1, 1, 0, 6)
                            if r == 4:
                                project_qk(b, h + 1, 1, 6, 12)
                            if r == 7 and h < HEADS - 2:
                                misc_free_of_qk(b, h + 1, 1)
                                project_qk(b, h + 2, 0, 0, 4)
                        if not last:
                            if n == 59:
                                pe.wait_ge(inv_stored, 8 * b + h)
                                project_qk(b + 1, 0, 0, 0, 6)
                            if n == 60:
                                project_qk(b + 1, 0, 0, 6, 12)
                            if n == 65:
                                misc_free_of_xhat(b + 1, TT - 1)
                                project_qk(b + 1, 0, 1, 0, 12)
                        if n == SLOTS + 2:
                            pe.wait_ge(turnA_stored, 64 * b + SLOTS)
                            spread_inv(b, HEADS - 1, turnA_bank)
                        if n == LAST_SLOT - 1 and not last:
                            pe.wait_ge(inv_stored, 8 * b + HEADS)
                            pe.wait_ge(turnB_stored, 64 * b + SLOTS)

                with pe.Fori(0, B - 1) as b:
                    entry(b, False)
                entry(B - 1, True)


def mix_pass(nc, x, o_scratch, w_out_raw, stage, b_out, gamma, beta, w_k, w_v, mu_r, mu_k, out, ln1_stats, ident):
    with ExitStack() as ctx:
        def sb(name, shape, dt=F32):
            return ctx.enter_context(nc.sbuf_tensor(name, shape, dt))

        def sem(name):
            return ctx.enter_context(nc.semaphore(name))

        CHUNK = T // 2
        NT = CHUNK // P
        CHUNKS = B * 2
        NAMES = ("out", "r", "k", "v")

        hi = {n: sb(f"mix_w{n}_hi", [P, KC, C], F32R) for n in NAMES}
        lo = {n: sb(f"mix_w{n}_lo", [P, KC, C], F32R) for n in NAMES}
        gam = sb("gam", [P, C])
        bet = sb("bet", [P, C])
        bo = sb("bo", [P, C])
        mu = {"k": sb("mu_k", [P, KC]), "r": sb("mu_r", [P, KC])}
        mu1 = {"k": sb("mu1_k", [P, KC]), "r": sb("mu1_r", [P, KC])}
        neg_half = sb("neg_half2", [P, NT])
        eps = sb("eps2", [P, NT])
        mean_x = sb("mean_x", [P, NT])
        xs = sb("xs", [P, NT, 2])
        o_raw = stage[:, 0]
        o_hi = sb("o_hi", [P, KC, CHUNK], F32R)
        o_lo = sb("o_lo", [P, KC, CHUNK], F32R)
        xc = sb("xc", [P, NT, C])
        y = sb("y", [P, NT, C])
        x2 = [sb("x2", [P, NT, C]), w_out_raw]
        bn6 = sb("bn6b", [P, NT, 6])
        mv_y = sb("mv_y", [P, NT, 2])
        mv_2 = sb("mv_2", [P, NT, 2])
        rstd_y = sb("rstd_y", [P, NT])
        rstd_2 = sb("rstd_2", [P, NT])
        lnT = sb("lnT", [P, KC, CHUNK + 1])
        mixed = stage[:, 1]
        m_hi = {n: sb(f"m{n}_hi", [P, KC, CHUNK], F32R) for n in "kr"}
        m_lo = {n: sb(f"m{n}_lo", [P, KC, CHUNK], F32R) for n in "kr"}
        relu = sb("relu", [P, 2, CHUNK])
        act_hi = sb("act_hi", [P, KC, CHUNK], F32R)
        act_lo = sb("act_lo", [P, KC, CHUNK], F32R)
        gate = sb("gate", [P, NT, C])
        raw = {"out": x2[1][:, :, :], "r": mixed[:, :, :], "k": x2[0][:, :, :], "v": gate[:, :, :]}

        bank = [ctx.enter_context(nc.psum_tensor(f"bank{i}", [P, C], F32)) for i in range(8)]
        ps_y, ps_k, ps_r, ps_v = bank[0:2], bank[2:4], bank[4:6], bank[6:8]
        ps_turn = ps_y + ps_r

        WEIGHT_TURNS = [(0, 2), (2, 4), (4, 6), (6, 12)]

        def weight_bank(u):
            return bank[2 + u % 6][:, :]

        w_in = {n: sem(f"w{n}_in") for n in ("k", "v", "small")}
        small_set = sem("small_set")
        w_turned = sem("w_turned")
        w_hi_done = sem("w_hi_done")
        w_lo_done = sem("w_lo_done")
        wo_split = sem("wo_split")
        o_in = sem("o_in")
        x_in = sem("xc_in")
        o_hi_done = sem("o_hi_done")
        o_lo_done = sem("o_lo_done")
        y_done = sem("y_done")
        y_stored = sem("y_stored")
        bn_step = sem("bn_step2")
        bn_y = sem("bn_y")
        eps_step = sem("eps_step")
        rstd_y_done = sem("rstd_y_done")
        xs_step = sem("xs_step")
        xs_done = sem("xs_done")
        res_act = sem("res_act")
        res_done = sem("res_done")
        t1_done = sem("t1_done")
        x2_done = sem("x2_done")
        bn2_step = sem("bn2_step")
        bn_2 = sem("bn_2")
        rstd_2_done = sem("rstd_2_done")
        ln2_done = sem("ln2_done")
        ln2_turned = sem("ln2_turned")
        prev_done = sem("prev_done")
        lnT_done = sem("lnT_done")
        before_done = {n: sem(f"before_{n}") for n in "kr"}
        mixed_done = {n: sem(f"mixed_{n}") for n in "kr"}
        m_hi_done = {n: sem(f"m_hi_{n}") for n in "kr"}
        m_lo_done = {n: sem(f"m_lo_{n}") for n in "kr"}
        k_done = sem("k_done")
        relu_done = sem("relu_done")
        act_hi_done = sem("act_hi_done")
        sq_done = sem("sq_done")
        act_lo_done = sem("act_lo_done")
        r_done = sem("r_done")
        gate_done = sem("gate_done")
        kv_done = sem("kv_done")
        rkv_done = sem("rkv_done")
        sum_done = sem("sum_done")
        out_done = sem("out_done")

        o_view = chunks_of(o_scratch)
        x_view = x.rearrange("b (c t p) n -> (b c) p t n", c=2, p=P)
        out_view = out.rearrange("b (c t p) n -> (b c) p t n", c=2, p=P)

        def spread(vec):
            return vec.rearrange("(o n) -> o n", o=1).broadcast_to([P, C])

        def over_steps(eng, step):
            step(0, 0, True, False)
            with eng.Fori(0, CHUNKS // 2 - 1) as i:
                step(2 * i + 1, 1, True, True)
                step(2 * i + 2, 0, True, True)
            step(CHUNKS - 1, 1, True, True)
            step(CHUNKS, 0, False, True)

        with nc.Block() as block:

            @block.sync
            def _(sp):
                def load_weight(n, w):
                    sp.dma_start(raw[n], w.rearrange("(k p) n -> p k n", p=P)).then_inc(w_in[n], 16)

                def load_o(g):
                    sp.dma_start(o_raw[:, :, :], o_view[g]).then_inc(o_in, 16)

                def load_x(g):
                    sp.dma_start(xc[:, :, :], x_view[g]).then_inc(x_in, 16)

                for dst, src in ((bo, b_out), (gam, gamma), (bet, beta)):
                    sp.dma_start(dst[:, :], spread(src)).then_inc(w_in["small"], 16)
                for dst, src in ((mu["k"], mu_k), (mu["r"], mu_r)):
                    sp.dma_start(dst[:, :], src.rearrange("(k p) -> p k", p=P),
                                 allow_slow_non_contiguous=True).then_inc(w_in["small"], 16)
                load_weight("k", w_k)
                load_weight("v", w_v)
                load_x(0)

                def step(g, par, first, second):
                    if first and not (isinstance(g, int) and g == CHUNKS - 1):
                        sp.wait_ge(o_lo_done, g + 1)
                        load_o(g + 1)
                        sp.wait_ge(x2_done, 4 * g + 4)
                        load_x(g + 1)
                    if second:
                        for t in range(NT):
                            sp.wait_ge(sum_done, 4 * g - 3 + t)
                            sp.dma_start(out_view[g - 1][:, t, :], gate[:, t, :]).then_inc(out_done, 16)

                over_steps(sp, step)
                sp.wait_ge(out_done, 16 * NT * CHUNKS + 16)

            @block.gpsimd
            def _(pool):
                pool.memset(eps[:, :], EPS).then_inc(eps_step, 1)
                pool.memset(neg_half[:, :], -0.5).then_inc(eps_step, 1)
                pool.wait_ge(eps_step, 2)
                pool.wait_ge(small_set, 2)

                def step(g, par, first, second):
                    if first:
                        pool.wait_ge(bn_y, g + 1)
                        pool.tensor_tensor(rstd_y[:, :], mv_y[:, :, 1], eps[:, :], ALU.add).then_inc(eps_step, 1)
                        pool.wait_ge(eps_step, 2 * g + 3)
                        pool.tensor_tensor(rstd_y[:, :], rstd_y[:, :], neg_half[:, :], ALU.pow).then_inc(rstd_y_done, 1)
                        for t in range(NT):
                            pool.wait_ge(res_act, 4 * g + t + 1)
                            pool.tensor_tensor(xc[:, t, :], xc[:, t, :], bet[:, :], ALU.add).then_inc(res_done, 1)
                        pool.wait_ge(bn_2, g + 1)
                        pool.tensor_tensor(rstd_2[:, :], mv_2[:, :, 1], eps[:, :], ALU.add).then_inc(eps_step, 1)
                        pool.wait_ge(eps_step, 2 * g + 4)
                        pool.tensor_tensor(rstd_2[:, :], rstd_2[:, :], neg_half[:, :], ALU.pow).then_inc(rstd_2_done, 1)
                    if second:
                        for t in range(NT):
                            pool.wait_ge(rkv_done, 4 * g - 3 + t)
                            pool.tensor_tensor(gate[:, t, :], gate[:, t, :], x2[1 - par][:, t, :],
                                               ALU.add).then_inc(sum_done, 1)

                over_steps(pool, step)

            @block.vector
            def _(dve):
                def weight_lo(u):
                    n, kc = ("r", "k", "v")[u // KC], u % KC
                    dve.wait_ge(w_hi_done, u + 1)
                    dve.tensor_tensor(lo[n][:, kc, :], weight_bank(u), f32(hi[n][:, kc, :]),
                                      ALU.subtract).then_inc(w_lo_done, 1)

                def residual_scales(g):
                    dve.tensor_scalar(xs[:, :, 0], ln1_stats[:, bass.ds(g * NT, NT), 1], RSQRT2, None,
                                      ALU.mult).then_inc(xs_step, 1)
                    dve.tensor_copy(mean_x[:, :], ln1_stats[:, bass.ds(g * NT, NT), 0]).then_inc(xs_step, 1)
                    dve.wait_ge(xs_step, 3 * g + 2)
                    dve.scalar_tensor_tensor(xs[:, :, 1], mean_x[:, :], -1.0, xs[:, :, 0], ALU.mult,
                                             ALU.mult).then_inc(xs_step, 1)
                    dve.wait_ge(xs_step, 3 * g + 3)
                    dve.tensor_scalar(xs[:, :, 0], xs[:, :, 0], 1.0, None, ALU.add).then_inc(xs_done, 1)

                def split_o(g):
                    dve.wait_ge(o_hi_done, g + 1)
                    dve.tensor_tensor(o_lo[:, :, :], o_raw[:, :, :], f32(o_hi[:, :, :]), ALU.subtract).then_inc(o_lo_done, 1)

                def store_y(g, t):
                    dve.wait_ge(y_done, 4 * g + t + 1)
                    dve.tensor_tensor(y[:, t, :], ps_y[t % 2][:, :], bo[:, :], ALU.add).then_inc(y_stored, 1)
                    dve.wait_ge(y_stored, 4 * g + t + 1)
                    dve.bn_stats(bn6[:, t, :], y[:, t, :]).then_inc(bn_step, 1)

                def aggregate(mv, done):
                    for t in range(NT):
                        ins = dve.bn_aggr(mv[:, t, :], bn6[:, t, :])
                    ins.then_inc(done, 1)

                def residual(g, par, t):
                    dve.scalar_tensor_tensor(y[:, t, :], y[:, t, :], mv_y[:, t, 0:1], gam[:, :], ALU.subtract,
                                             ALU.mult).then_inc(t1_done, 1)
                    dve.wait_ge(res_done, 4 * g + t + 1)
                    dve.wait_ge(t1_done, 4 * g + t + 1)
                    dve.scalar_tensor_tensor(x2[par][:, t, :], y[:, t, :], rstd_y[:, t:t + 1], xc[:, t, :], ALU.mult,
                                             ALU.add).then_inc(x2_done, 1)
                    dve.wait_ge(x2_done, 4 * g + t + 1)
                    dve.bn_stats(bn6[:, t, :], x2[par][:, t, :]).then_inc(bn2_step, 1)

                def activation_lo(f, d):
                    dve.wait_ge(act_hi_done, 4 * f + d + 1)
                    dve.tensor_tensor(relu[:, d % 2, :], relu[:, d % 2, :], relu[:, d % 2, :], ALU.mult).then_inc(sq_done, 1)
                    dve.wait_ge(sq_done, 4 * f + d + 1)
                    dve.tensor_tensor(act_lo[:, d, :], relu[:, d % 2, :], f32(act_hi[:, d, :]),
                                      ALU.subtract).then_inc(act_lo_done, 1)

                def gated(f, t):
                    dve.wait_ge(kv_done, 4 * f + t + 1)
                    dve.wait_ge(gate_done, 4 * f + t + 1)
                    dve.tensor_tensor(gate[:, t, :], ps_v[t % 2][:, :], gate[:, t, :], ALU.mult).then_inc(rkv_done, 1)

                def mix(g, n):
                    for kc in range(KC):
                        dve.wait_ge(before_done[n], 4 * g + kc + 1)
                        dve.scalar_tensor_tensor(mixed[:, kc, :], lnT[:, kc, 1:CHUNK + 1], mu[n][:, kc:kc + 1],
                                                 mixed[:, kc, :], ALU.mult, ALU.add).then_inc(mixed_done[n], 1)

                def mix_lo(g, n):
                    for kc in range(KC):
                        dve.wait_ge(m_hi_done[n], 4 * g + kc + 1)
                        dve.tensor_tensor(m_lo[n][:, kc, :], mixed[:, kc, :], f32(m_hi[n][:, kc, :]),
                                          ALU.subtract).then_inc(m_lo_done[n], 1)

                dve.wait_ge(wo_split, 1)
                dve.tensor_tensor(lo["out"][:, :, :], raw["out"], f32(hi["out"][:, :, :]),
                                  ALU.subtract).then_inc(wo_split, 1)
                residual_scales(0)
                split_o(0)
                dve.wait_ge(w_in["small"], 80)
                dve.tensor_scalar(gam[:, :], gam[:, :], RSQRT2, None, ALU.mult).then_inc(small_set, 1)
                dve.tensor_scalar(bet[:, :], bet[:, :], RSQRT2, None, ALU.mult).then_inc(small_set, 1)
                for n in "kr":
                    dve.tensor_scalar(mu1[n][:, :], mu[n][:, :], -1.0, 1.0, ALU.mult, ALU.add).then_inc(small_set, 1)
                dve.memset(lnT[:, :, 0:1], 0.0).then_inc(out_done, 16)

                def step(g, par, first, second):
                    f = g - 1
                    if first:
                        for t in range(NT):
                            store_y(g, t)
                            if t == 1 and second:
                                mix_lo(f, "r")
                            if t < 3 and not second:
                                for u in range(*WEIGHT_TURNS[t]):
                                    weight_lo(u)
                        dve.wait_ge(bn_step, 4 * g + 4)
                    if second:
                        if not first:
                            mix_lo(f, "r")
                        activation_lo(f, 0)
                    if first:
                        aggregate(mv_y, bn_y)
                    if not second:
                        for u in range(6, 8):
                            weight_lo(u)
                    if second:
                        activation_lo(f, 1)
                    if first:
                        dve.wait_ge(rstd_y_done, g + 1)
                    for t in range(NT):
                        if first:
                            residual(g, par, t)
                        if first and t == 3:
                            dve.wait_ge(bn2_step, 4 * g + 4)
                        if second and t >= 2:
                            activation_lo(f, t)
                        if first and t == 3:
                            aggregate(mv_2, bn_2)
                    if not second:
                        for u in range(8, 10):
                            weight_lo(u)
                    more = first and not (isinstance(g, int) and g == CHUNKS - 1)
                    if more:
                        residual_scales(g + 1)
                    if first:
                        if par == 1:
                            dve.tensor_copy(lnT[:, :, 0:1], lnT[:, :, CHUNK:CHUNK + 1]).then_inc(prev_done, 1)
                        else:
                            dve.memset(lnT[:, :, 0:1], 0.0).then_inc(prev_done, 1)
                        dve.wait_ge(rstd_2_done, g + 1)
                        for t in range(NT):
                            dve.tensor_scalar(y[:, t, :], x2[par][:, t, :], mv_2[:, t, 0:1], rstd_2[:, t:t + 1],
                                              ALU.subtract, ALU.mult).then_inc(ln2_done, 1)
                    if more:
                        split_o(g + 1)
                    if not second:
                        for u in range(10, 12):
                            weight_lo(u)
                    if second:
                        gated(f, 0)
                    if first:
                        mix(g, "k")
                    if second:
                        gated(f, 1)
                    if first:
                        mix_lo(g, "k")
                    if second:
                        gated(f, 2)
                    if first:
                        mix(g, "r")
                    if second:
                        gated(f, 3)

                over_steps(dve, step)

            @block.scalar
            def _(act):
                def weight_hi(u):
                    n, kc = ("r", "k", "v")[u // KC], u % KC
                    act.wait_ge(w_turned, u + 1)
                    act.activation(hi[n][:, kc, :], weight_bank(u), ACT.Copy).then_inc(w_hi_done, 1)

                def split_o(g):
                    if not (isinstance(g, int) and g == 0):
                        act.wait_ge(o_in, 16 * g)
                    act.activation(o_hi[:, :, :], o_raw[:, :, :], ACT.Copy).then_inc(o_hi_done, 1)

                def mix_before(g, n, kc):
                    act.activation(mixed[:, kc, :], lnT[:, kc, 0:CHUNK], ACT.Copy,
                                   scale=mu1[n][:, kc:kc + 1]).then_inc(before_done[n], 1)

                def mix_hi(g, n, kc):
                    act.wait_ge(mixed_done[n], 4 * g + kc + 1)
                    act.activation(m_hi[n][:, kc, :], mixed[:, kc, :], ACT.Copy).then_inc(m_hi_done[n], 1)

                act.activation(hi["out"][:, :, :], raw["out"], ACT.Copy).then_inc(wo_split, 1)
                split_o(0)

                def step(g, par, first, second):
                    f = g - 1
                    if not second:
                        for u in range(3 * KC):
                            weight_hi(u)
                    if first:
                        act.wait_ge(x_in, 16 * g + 16)
                        act.wait_ge(xs_done, g + 1)
                        for t in range(NT):
                            act.activation(xc[:, t, :], xc[:, t, :], ACT.Identity, scale=xs[:, t, 0:1],
                                           bias=xs[:, t, 1:2]).then_inc(res_act, 1)
                    if second:
                        for d in range(KC):
                            act.wait_ge(k_done, 4 * f + d + 1)
                            if d >= 2:
                                act.wait_ge(act_lo_done, 4 * f + d - 1)
                            act.activation(relu[:, d % 2, :], ps_k[d % 2][:, :], ACT.Relu).then_inc(relu_done, 1)
                            act.wait_ge(relu_done, 4 * f + d + 1)
                            act.activation(act_hi[:, d, :], relu[:, d % 2, :], ACT.Square).then_inc(act_hi_done, 1)
                    if first and not (isinstance(g, int) and g == CHUNKS - 1):
                        act.wait_ge(y_done, 4 * g + 4)
                        split_o(g + 1)
                    if second:
                        for t in range(NT):
                            act.wait_ge(r_done, 4 * f + t + 1)
                            act.wait_ge(out_done, 64 * f + 16)
                            act.activation(gate[:, t, :], ps_r[t % 2][:, :], ACT.Sigmoid).then_inc(gate_done, 1)
                    if first:
                        for t in range(NT):
                            act.wait_ge(ln2_turned, 4 * g + t + 1)
                            if t == 0:
                                act.wait_ge(prev_done, g + 1)
                            act.activation(lnT[:, :, 1 + t * P:1 + (t + 1) * P],
                                           ps_turn[t][:, :].rearrange("p (k n) -> p k n", k=KC),
                                           ACT.Copy).then_inc(lnT_done, 1)
                        act.wait_ge(lnT_done, 4 * g + 4)
                        for kc in range(KC):
                            mix_before(g, "k", kc)
                        for kc in range(KC):
                            mix_hi(g, "k", kc)
                        for kc in range(KC):
                            act.wait_ge(m_lo_done["k"], 4 * g + kc + 1)
                            mix_before(g, "r", kc)
                        for kc in range(KC):
                            mix_hi(g, "r", kc)

                over_steps(act, step)

            @block.tensor
            def _(pe):
                def turn_weight(u):
                    n, kc = ("r", "k", "v")[u // KC], u % KC
                    if n != "r":
                        pe.wait_ge(w_in[n], 16)
                    if u >= 6:
                        pe.wait_ge(w_lo_done, u - 5)
                    for d in range(KC):
                        ins = pe.transpose(weight_bank(u)[:, d * P:(d + 1) * P], raw[n][:, d, kc * P:(kc + 1) * P],
                                           ident[:, :])
                    ins.then_inc(w_turned, 1)

                def product(out, a_hi, a_lo, b_hi, b_lo, a_cols, b_cols, done):
                    prods = [(a, b, kc) for kc in range(KC) for a, b in ((a_lo, b_hi), (a_hi, b_lo), (a_hi, b_hi))]
                    for i, (a, b, kc) in enumerate(prods):
                        ins = pe.matmul(out, a[:, kc, a_cols], b[:, kc, b_cols], start=(i == 0), stop=(i == len(prods) - 1))
                    ins.then_inc(done, 1)

                whole = slice(0, C)

                def value_product(f, t):
                    if t >= 2:
                        pe.wait_ge(rkv_done, 4 * f + t - 1)
                    product(ps_v[t % 2][:, :], act_hi, act_lo, hi["v"], lo["v"], slice(t * P, (t + 1) * P), whole, kv_done)

                def step(g, par, first, second):
                    f = g - 1
                    if not second:
                        pe.wait_ge(wo_split, 2)
                    if first:
                        pe.wait_ge(o_hi_done, g + 1)
                        pe.wait_ge(o_lo_done, g + 1)
                        for t in range(NT):
                            if t < 2 and second:
                                pe.wait_ge(lnT_done, 4 * g - 3 + t)
                            if t >= 2:
                                pe.wait_ge(y_stored, 4 * g + t - 1)
                            product(ps_y[t % 2][:, :], o_hi, o_lo, hi["out"], lo["out"], slice(t * P, (t + 1) * P), whole, y_done)
                            if not second:
                                for u in range(*WEIGHT_TURNS[t]):
                                    turn_weight(u)
                    if second:
                        pe.wait_ge(m_hi_done["k"], 4 * f + 4)
                        pe.wait_ge(m_lo_done["k"], 4 * f + 4)
                        for d in range(KC):
                            if d >= 2:
                                pe.wait_ge(relu_done, 4 * f + d - 1)
                            product(ps_k[d % 2][:, :], hi["k"], lo["k"], m_hi["k"], m_lo["k"], slice(d * P, (d + 1) * P), whole, k_done)
                        pe.wait_ge(m_hi_done["r"], 4 * f + 4)
                        pe.wait_ge(m_lo_done["r"], 4 * f + 4)
                        for t in range(NT):
                            if t >= 2:
                                pe.wait_ge(gate_done, 4 * f + t - 1)
                            product(ps_r[t % 2][:, :], m_hi["r"], m_lo["r"], hi["r"], lo["r"], slice(t * P, (t + 1) * P), whole, r_done)
                        pe.wait_ge(act_lo_done, 4 * f + 4)
                        value_product(f, 0)
                    if first:
                        for t in range(NT):
                            pe.wait_ge(ln2_done, 4 * g + t + 1)
                            if t < 2:
                                pe.wait_ge(y_stored, 4 * g + t + 3)
                            elif second:
                                pe.wait_ge(gate_done, 4 * f + t + 1)
                            else:
                                pe.wait_ge(w_lo_done, 10)
                            for k in range(KC):
                                ins = pe.transpose(ps_turn[t][:, k * P:(k + 1) * P], y[:, t, k * P:(k + 1) * P], ident[:, :])
                            ins.then_inc(ln2_turned, 1)
                    if second:
                        for t in range(1, NT):
                            value_product(f, t)
                    if not second:
                        pe.wait_ge(w_lo_done, 3 * KC)

                over_steps(pe, step)


def seq_preln_block(nc, x, w_qk, b_qk, w_v, b_v, w_out, b_out, gamma, beta, w_r, w_k, w_v2, mu_r, mu_k, out):
    with ExitStack() as ctx:
        ident = ctx.enter_context(nc.sbuf_tensor("ident", [P, P], F32))
        ln1_stats = ctx.enter_context(nc.sbuf_tensor("ln1_stats", [P, B * TT, 2], F32))
        stage = ctx.enter_context(nc.sbuf_tensor("stage", [P, 2, KC, C], F32))
        w_out_raw = ctx.enter_context(nc.sbuf_tensor("w_out_raw", [P, KC, C], F32))
        o_scratch = nc.dram_tensor("o_scratch", [B, 2, HEADS, DH, HALF], F32, kind="Internal").ap()
        attention_pass(nc, x, w_qk, b_qk, w_v, b_v, w_out, w_r, w_out_raw, stage, o_scratch, ln1_stats, ident)
        mix_pass(nc, x, o_scratch, w_out_raw, stage, b_out, gamma, beta, w_k, w_v2, mu_r, mu_k, out, ln1_stats, ident)


_INS = ["L0_attn_x", "L0_attn_W_qk", "L0_attn_b_qk", "L0_attn_W_v", "L0_attn_b_v", "L0_attn_W_out", "L0_attn_b_out",
        "L0_attn_ln_gamma", "L0_attn_ln_beta", "L0_ffn_W_r", "L0_ffn_W_k", "L0_ffn_W_v", "L0_ffn_mu_r", "L0_ffn_mu_k"]


def kernel(**inputs):
    import numpy as _np
    import concourse.bacc as _bacc
    from concourse import mybir as _mybir
    from concourse.bass_utils import run_bass_kernel_spmd as _run

    nc = _bacc.Bacc("TRN2", target_bir_lowering=False, num_devices=1)
    arrays, args = {}, []
    for name in _INS:
        a = _np.ascontiguousarray(inputs[name])
        arrays[f"in_{name}_dram"] = a
        args.append(nc.dram_tensor(f"in_{name}_dram", a.shape, _mybir.dt.from_np(a.dtype), kind="ExternalInput").ap())
    args.append(nc.dram_tensor("out_dram", [B, T, C], F32, kind="ExternalOutput").ap())
    seq_preln_block(nc, *args)
    r = _run(nc, [arrays], core_ids=[0])
    return r.results[0]["out_dram"]
```
